# Optimizing a Trainium2 kernel written in Bass

```python
import numpy as np
import jax
import jax.numpy as jnp

def _softmax(x, axis=-1):
    return jax.nn.softmax(x, axis=axis)

def _gelu(x):
    return jax.nn.gelu(x, approximate=True)

def _silu(x):
    return jax.nn.silu(x)

def _sigmoid(x):
    return jax.nn.sigmoid(x)

def _layernorm(x, axis=-1, eps=1e-05):
    m = jnp.mean(x, axis=axis, keepdims=True)
    v = jnp.var(x, axis=axis, keepdims=True)
    return (x - m) / jnp.sqrt(v + eps)

def _scatter_add(tgt, idx, src, axis=0):
    return tgt.at[idx].add(src)

def _segment_sum(src, seg, n):
    return jax.ops.segment_sum(src, seg, n)
kernel_name = 'mk_decoder_preln_d1_seqx_r8_1f55f2'

def setup_inputs(seed: int=0):
    np.random.seed(seed)
    _w = jnp.asarray

    def _rec_inputs():
        import jax
        import jax.numpy as jnp
        _rk = jax.random.key(seed)
        x = 7.22e-05 + 1 * jax.random.normal(jax.random.fold_in(_rk, 1), (4, 256, 256), jnp.float32)
        _lenS = 256 - jax.random.randint(jax.random.fold_in(_rk, 7), (4,), 0, max(1, 256 // 4) + 1, jnp.int32)
        _lenS2 = 1601 - jax.random.randint(jax.random.fold_in(_rk, 8), (4,), 0, max(1, 1601 // 4) + 1, jnp.int32)
        _ctx_512P = jax.random.normal(jax.random.fold_in(_rk, 11), (4, 16, 64), jnp.float32)
        _ctx_512c = jax.random.dirichlet(jax.random.fold_in(_rk, 511), 0.3 * jnp.ones((16,), jnp.float32), (4, 1601))
        _ctx_512t = jnp.einsum('bsk,bkd->bsd', _ctx_512c, _ctx_512P)
        _ctx_512t = _ctx_512t * jax.lax.rsqrt(jnp.mean(jnp.square(_ctx_512t)) + 1e-12) * 0.953939
        ctx_512 = -0.000514642 + 1.00011 * (_ctx_512t + 0.3 * jax.random.normal(jax.random.fold_in(_rk, 611), (4, 1601, 64), jnp.float32))
        return (x, ctx_512)
    x, ctx_512 = _rec_inputs()

    def _L0_attn_setup():
        import jax, jax.numpy as jnp
        import numpy as np
        H = 32
        KV = 8
        D = 64
        WIN = 64
        BASE = 10000.0

        def _rope_tables(S):
            inv_freq = 1.0 / BASE ** (jnp.arange(0, D, 2, dtype=jnp.float32) / D)
            t = jnp.arange(S, dtype=jnp.float32)
            freqs = t[:, None] * inv_freq[None, :]
            emb = jnp.concatenate([freqs, freqs], axis=-1)
            return (jnp.cos(emb)[:, None, :], jnp.sin(emb)[:, None, :])

        def _rotate_half(u):
            return jnp.concatenate([-u[..., D // 2:], u[..., :D // 2]], axis=-1)
        key = jax.random.key(seed)
        ks = jax.random.split(key, 5)
        B, S, DIM = (2, 256, 256)
        x = jax.random.normal(ks[0], (B, S, DIM), dtype=jnp.float32)
        wq = jax.random.normal(ks[1], (H * D, DIM), dtype=jnp.float32) * 0.02
        wk = jax.random.normal(ks[2], (KV * D, DIM), dtype=jnp.float32) * 0.02
        wv = jax.random.normal(ks[3], (KV * D, DIM), dtype=jnp.float32) * 0.02
        wo = jax.random.normal(ks[4], (DIM, H * D), dtype=jnp.float32) * 0.02
        return {'x': x, 'wq': wq, 'wk': wk, 'wv': wv, 'wo': wo}
    _L0_attn_all = _L0_attn_setup()
    _L0_attn_in = {k: v for k, v in _L0_attn_all.items() if k in ('wq', 'wk', 'wv', 'wo')}
    del _L0_attn_all

    def _L0_xattn_setup():
        import jax, jax.numpy as jnp
        import numpy as np
        B, S, H, NH, L = (2, 256, 256, 16, 64)
        HD = H // NH
        key = jax.random.key(seed)
        k1, k2, k3, k4, k5 = jax.random.split(key, 5)
        scale = 0.02
        return {'q': jax.random.normal(k1, (B, S, H), dtype=jnp.float32), 'latent_kv': jax.random.normal(k2, (B, S, L), dtype=jnp.float32), 'Wq': jax.random.normal(k3, (H, H), dtype=jnp.float32) * scale, 'Wkv_expand': jax.random.normal(k4, (2 * H, L), dtype=jnp.float32) * scale, 'Wout': jax.random.normal(k5, (H, H), dtype=jnp.float32) * scale}
    _L0_xattn_all = _L0_xattn_setup()
    _L0_xattn_in = {k: v for k, v in _L0_xattn_all.items() if k in ('Wq', 'Wkv_expand', 'Wout')}
    del _L0_xattn_all

    def _L0_ffn_setup():
        import jax, jax.numpy as jnp
        import numpy as np

        def _sparsify_2to4(h):
            B, S, I = h.shape
            g = h.reshape(B, S, I // 4, 4)
            a = jnp.abs(g)
            _, idx = jax.lax.top_k(a, 2)
            pos = jnp.arange(4)
            mask = (pos == idx[..., 0:1]) | (pos == idx[..., 1:2])
            return (g * mask.astype(g.dtype)).reshape(B, S, I)
        key = jax.random.key(seed)
        k1, k2, k3, k4 = jax.random.split(key, 4)
        B, S, H, I = (4, 256, 256, 1024)
        x = jax.random.normal(k1, (B, S, H), dtype=jnp.float32)
        w_gate = jax.random.normal(k2, (H, I), dtype=jnp.float32) / np.sqrt(H)
        w_up = jax.random.normal(k3, (H, I), dtype=jnp.float32) / np.sqrt(H)
        w_down = jax.random.normal(k4, (I, H), dtype=jnp.float32) / np.sqrt(I)
        return {'x': x, 'w_gate': w_gate, 'w_up': w_up, 'w_down': w_down}
    _L0_ffn_all = _L0_ffn_setup()
    _L0_ffn_in = {k: v for k, v in _L0_ffn_all.items() if k in ('w_gate', 'w_up', 'w_down')}
    del _L0_ffn_all
    return {'x': x, 'ctx_512': ctx_512, 'L0_attn_wq': _L0_attn_in['wq'], 'L0_attn_wk': _L0_attn_in['wk'], 'L0_attn_wv': _L0_attn_in['wv'], 'L0_attn_wo': _L0_attn_in['wo'], 'L0_xattn_Wq': _L0_xattn_in['Wq'], 'L0_xattn_Wkv_expand': _L0_xattn_in['Wkv_expand'], 'L0_xattn_Wout': _L0_xattn_in['Wout'], 'L0_ffn_w_gate': _L0_ffn_in['w_gate'], 'L0_ffn_w_up': _L0_ffn_in['w_up'], 'L0_ffn_w_down': _L0_ffn_in['w_down']}

def reference(x, ctx_512, L0_attn_wq, L0_attn_wk, L0_attn_wv, L0_attn_wo, L0_xattn_Wq, L0_xattn_Wkv_expand, L0_xattn_Wout, L0_ffn_w_gate, L0_ffn_w_up, L0_ffn_w_down):
    import jax
    import jax.numpy as jnp

    def _L0_attn_ref(x, wq, wk, wv, wo):
        import jax, jax.numpy as jnp
        import numpy as np
        H = 32
        KV = 8
        D = 64
        WIN = 64
        BASE = 10000.0

        def _rope_tables(S):
            inv_freq = 1.0 / BASE ** (jnp.arange(0, D, 2, dtype=jnp.float32) / D)
            t = jnp.arange(S, dtype=jnp.float32)
            freqs = t[:, None] * inv_freq[None, :]
            emb = jnp.concatenate([freqs, freqs], axis=-1)
            return (jnp.cos(emb)[:, None, :], jnp.sin(emb)[:, None, :])

        def _rotate_half(u):
            return jnp.concatenate([-u[..., D // 2:], u[..., :D // 2]], axis=-1)
        B, S, _ = x.shape
        q = (x @ wq.T).reshape(B, S, H, D)
        k = (x @ wk.T).reshape(B, S, KV, D)
        v = (x @ wv.T).reshape(B, S, KV, D)
        cos, sin = _rope_tables(S)
        q = q * cos + _rotate_half(q) * sin
        k = k * cos + _rotate_half(k) * sin
        q = q.transpose(0, 2, 1, 3)
        k = jnp.repeat(k.transpose(0, 2, 1, 3), H // KV, axis=1)
        v = jnp.repeat(v.transpose(0, 2, 1, 3), H // KV, axis=1)
        scale = 1.0 / jnp.sqrt(jnp.float32(D))
        scores = jnp.einsum('bhqd,bhkd->bhqk', q, k) * scale
        i = jnp.arange(S)[:, None]
        j = jnp.arange(S)[None, :]
        window_mask = jnp.abs(i - j) > WIN // 2
        causal_mask = j > i
        masked = window_mask | causal_mask
        scores = jnp.where(masked[None, None], -jnp.inf, scores)
        attn = jax.nn.softmax(scores, axis=-1)
        out = jnp.einsum('bhqk,bhkd->bhqd', attn, v)
        out = out.transpose(0, 2, 1, 3).reshape(B, S, H * D)
        return out @ wo.T

    def _L0_xattn_ref(q, latent_kv, Wq, Wkv_expand, Wout):
        import jax, jax.numpy as jnp
        import numpy as np
        B, S, H, NH, L = (2, 256, 256, 16, 64)
        HD = H // NH
        b, sq, _ = q.shape
        sk = latent_kv.shape[1]
        qp = q @ Wq.T
        kv = latent_kv @ Wkv_expand.T
        k, v = jnp.split(kv, 2, axis=-1)
        qh = qp.reshape(b, sq, NH, HD).transpose(0, 2, 1, 3)
        kh = k.reshape(b, sk, NH, HD).transpose(0, 2, 1, 3)
        vh = v.reshape(b, sk, NH, HD).transpose(0, 2, 1, 3)
        inv_sqrt_d = 1.0 / jnp.sqrt(jnp.float32(HD))
        scores = jnp.einsum('bhqd,bhkd->bhqk', qh, kh) * inv_sqrt_d
        causal = jnp.tril(jnp.ones((sq, sk), dtype=bool))
        scores = jnp.where(causal, scores, jnp.finfo(scores.dtype).min)
        attn = jax.nn.softmax(scores, axis=-1)
        out = jnp.einsum('bhqk,bhkd->bhqd', attn, vh)
        out = out.transpose(0, 2, 1, 3).reshape(b, sq, H)
        return out @ Wout.T

    def _L0_ffn_ref(x, w_gate, w_up, w_down):
        import jax, jax.numpy as jnp
        import numpy as np

        def _sparsify_2to4(h):
            B, S, I = h.shape
            g = h.reshape(B, S, I // 4, 4)
            a = jnp.abs(g)
            _, idx = jax.lax.top_k(a, 2)
            pos = jnp.arange(4)
            mask = (pos == idx[..., 0:1]) | (pos == idx[..., 1:2])
            return (g * mask.astype(g.dtype)).reshape(B, S, I)
        h = jax.nn.silu(jnp.einsum('bsh,hi->bsi', x, w_gate)) * jnp.einsum('bsh,hi->bsi', x, w_up)
        h_sparse = _sparsify_2to4(h)
        return jnp.einsum('bsi,ih->bsh', h_sparse, w_down)
    x = x + _L0_attn_ref(_layernorm(x, axis=-1), L0_attn_wq, L0_attn_wk, L0_attn_wv, L0_attn_wo)
    x = x + _L0_xattn_ref(_layernorm(x, axis=-1), ctx_512, L0_xattn_Wq, L0_xattn_Wkv_expand, L0_xattn_Wout)
    x = x + _L0_ffn_ref(_layernorm(x, axis=-1), L0_ffn_w_gate, L0_ffn_w_up, L0_ffn_w_down)
    return x

_drawn_inputs = setup_inputs


def setup_inputs(seed=0):
    import zlib

    import numpy as np

    out = dict(_drawn_inputs(seed))
    spreads = {}
    factors = {'L0_attn_wq': 4.545, 'L0_attn_wk': 4.394, 'L0_xattn_Wq': 41.962}
    for name, (base, spread) in spreads.items():
        noise = np.random.default_rng([zlib.crc32(name.encode()), seed]).standard_normal(out[name].shape)
        drawn = base * np.exp(spread * noise) if base else spread * noise
        out[name] = jnp.asarray(drawn.astype(out[name].dtype))
    for name, factor in factors.items():
        out[name] = (out[name] * factor).astype(out[name].dtype)
    return out
```

```python
from contextlib import ExitStack

import numpy as np

import concourse.bass as bass
from concourse import mybir

ALU = mybir.AluOpType
ACT = mybir.ActivationFunctionType
AX = mybir.AxisListType
F32 = mybir.dt.float32
BF16 = mybir.dt.bfloat16

P = 128
B, S, D = 4, 256, 256
KT = D // P
TT = S // P
H, KV, HD = 32, 8, 64
R = H // KV
HALF = HD // 2
WIN = 32
QB = 32
NQB = S // QB
WK = QB + WIN
PAIRS = KV // 2
GROUPS = KV // 4
QG = GROUPS * R
RG = QG + GROUPS
XH, XD, L = 16, 16, 64
HG = XH * XD // P
HPT = P // XD
XU0, XU1 = 4, 8
XU = XU0 + XU1
UNITS = NQB + XU
FF = 1024
FC = FF // (4 * P)
EPS = 1e-5
MASKED = -1.0e37
LAG_T, LAG_V = 2, 3
ND = 4

BANK_S, BANK_PT, BANK_O, BANK_M = 0, 2, 4, 5
NM = 3

FIRST_USES = ["ln1", "k0", "k1", "v0", "v1"] + [f"q{g}" for g in range(QG)]
USES = (["ln1", "k2", "v2", "wo", "k0", "k1", "v0", "ln2", "v1", "q2", "q0", "q1", "q2n",
         "out", "q3", "q4", "q5", "ln3", "q6", "q7"]
        + [f"{w}{c}{j}" for c in range(FC) for j in range(2) for w in ("gate", "up")]
        + ["down"])
QNAME = ["q0", "q1", "q2n", "q3", "q4", "q5", "q6", "q7"]
FIRST_USES = ["ln1", "k0", "k1", "v0", "v1"] + QNAME


LAST_USES = [u for u in USES if u not in FIRST_USES]


def ring_use(name, b):
    if b is None:
        n = FIRST_USES.index(name)
        return n % NM, n // NM
    last = isinstance(b, int) and b == B - 1
    n = (LAST_USES if last else USES).index(name)
    before = len([m for m in range(len(FIRST_USES)) if m % NM == n % NM])
    per = len([m for m in range(len(USES)) if m % NM == n % NM])
    return n % NM, b * per + (before + n // NM)


def pool_sums(n):
    batches, m = divmod(n, RG)
    return batches * (4 * GROUPS + 2 * QG) + (4 * m if m <= GROUPS else 4 * GROUPS + 2 * (m - GROUPS))


def build(nc, x, ctxT, wqk, wv, wo, xwq, xwk, xwv, xwo, wgu, wd, trig, masks, ident, rowmask, out):
    es = ExitStack()
    with es:
        def sb(name, shape, dt=F32):
            return es.enter_context(nc.sbuf_tensor(name, shape, dt))

        def sem(name):
            return es.enter_context(nc.semaphore(name))

        wqk_sb = sb("wqk_sb", [P, KT, RG, 2, P])
        wv_sb = sb("wv_sb", [P, KT, KV * HD])
        wo_sb = sb("wo_sb", [P, PAIRS, R, D])
        xwq_sb = sb("xwq_sb", [P, KT, D])
        xwk_sb = sb("xwk_sb", [L, D])
        xwv_sb = sb("xwv_sb", [L, D])
        xwo_sb = sb("xwo_sb", [P, HG, D])
        wgu_sb = sb("wgu_sb", [P, KT, 2, FC * 4, P])
        wd_sb = sb("wd_sb", [P, FC * 4, D])
        trig_sb = sb("trig_sb", [P, 3, S])
        mask_sb = sb("mask_sb", [P, 4, 512], BF16)
        ident_sb = sb("ident_sb", [P, P])
        ident_bf = sb("ident_bf", [P, P], BF16)
        rowmask_sb = sb("rowmask_sb", [P, HPT])
        power = sb("power", [P, TT])
        x_ln = sb("x_ln", [P, TT, D])
        x_res = sb("x_res", [P, TT, D])
        x1 = sb("x1", [P, TT, D])
        x2 = sb("x2", [P, TT, D])
        y = sb("y", [P, TT, D])
        stats = sb("stats", [P, 3, TT, 6])
        moments = sb("moments", [P, 3, TT, 2])
        vareps = sb("vareps", [P, 3, TT])
        rstd = sb("rstd", [P, 3, TT])
        xn = sb("xn", [P, 3, TT, D])
        xnT = sb("xnT", [P, 3, KT, S])
        rope = sb("rope", [P, 2, 2, 2, S])
        qs = sb("qs", [P, PAIRS, S, R])
        qs_rows = qs[:].rearrange("p c s r -> p c (s r)")
        kd = sb("kd", [P, PAIRS, 2, WIN + S])
        vb = sb("vb", [P, NQB, PAIRS, 2 * HD])
        prob = sb("prob", [P, ND, 512])
        mx = sb("mx", [P, ND, 8])
        total = sb("total", [P, ND, 8])
        inv = sb("inv", [P, ND, 8])
        pT = sb("pT", [P, 2, 512])
        ctx_sb = sb("ctx_sb", [L, S])
        k2T = sb("k2T", [P, HG, S])
        k2d = sb("k2d", [P, HG, HPT, S])
        v2z = sb("v2z", [P, TT, XH, 2 * XD])
        q2T = sb("q2T", [P, HG, S])
        o2T = sb("o2T", [P, HG, S])
        hidden = sb("hidden", [P, FC, 4, S])
        mask_f = hidden[:].rearrange("p c j s -> p (c j s)").rearrange("p (m n) -> p m n", m=4)
        mag = sb("mag", [P, 4, S])
        beats = sb("beats", [P, 6, S], BF16)
        part = sb("part", [P, 4, S], BF16)
        wins = sb("wins", [P, 4, S], BF16)

        ps = es.enter_context(nc.psum_tensor("ps", [P, 8, 512], F32))

        s_const = sem("s_const")
        s_wqk = sem("s_wqk")
        s_wv = sem("s_wv")
        s_wrest = [sem(f"s_w{n}") for n in ("wo", "xattn", "gu", "d")]
        s_wo, s_xw, s_wgu, s_wd = s_wrest
        s_xln = sem("s_xln")
        s_xres = sem("s_xres")
        s_ctx = sem("s_ctx")
        s_zero = sem("s_zero")
        s_cbf = sem("s_cbf")
        s_filled = [sem(f"s_filled{k}") for k in range(NM)]
        s_drained = [sem(f"s_drained{k}") for k in range(NM)]
        s_stats = sem("s_stats")
        s_mom = sem("s_mom")
        s_var = sem("s_var")
        s_rstd = sem("s_rstd")
        s_xn = sem("s_xn")
        s_addP = sem("s_addP")
        s_addV = sem("s_addV")
        s_score = sem("s_score")
        s_max = sem("s_max")
        s_sub = sem("s_sub")
        s_exp = sem("s_exp")
        s_sum = sem("s_sum")
        s_inv = sem("s_inv")
        s_norm = sem("s_norm")
        s_tr = sem("s_tr")
        s_pT = sem("s_pT")
        s_av = sem("s_av")
        s_oT = sem("s_oT")
        s_k2a = sem("s_k2a")
        s_k2p = sem("s_k2p")
        s_o2T = sem("s_o2T")
        s_mag = sem("s_mag")
        s_beats = sem("s_beats")
        s_part = sem("s_part")
        s_wins = sem("s_wins")
        s_kept = sem("s_kept")
        s_out = sem("s_out")

        def bank(name, b):
            k, _ = ring_use(name, b)
            return ps[:, BANK_M + k, :]

        def half_banks(name, b):
            return bank(name, b).rearrange("p (t n) -> p t n", t=2)

        def wait_filled(eng, name, b):
            k, n = ring_use(name, b)
            eng.wait_ge(s_filled[k], n + 1)

        def wait_drained(eng, name, b):
            k, n = ring_use(name, b)
            eng.wait_ge(s_drained[k], n + 1)

        def wait_before(eng, name, b):
            wait_drained(eng, name, b - 1 if not isinstance(b, int) or b else None)

        def filled(name, b):
            return s_filled[ring_use(name, b)[0]]

        def drained(name, b):
            return s_drained[ring_use(name, b)[0]]

        block = es.enter_context(nc.Block())

        @block.sync
        def _(sp):
            def load_x(b):
                return x[b].rearrange("(t p) d -> p t d", p=P)

            sp.dma_start(x_ln[:], load_x(0)).then_inc(s_xln, 16)
            sp.dma_start(ident_sb[:], ident).then_inc(s_const, 16)
            for g in (QG, QG + 1):
                sp.dma_start(wqk_sb[:, :, g], wqk[:, :, g]).then_inc(s_wqk, 16)
            sp.dma_start(trig_sb[:], trig).then_inc(s_const, 16)
            sp.dma_start(wv_sb[:], wv).then_inc(s_wv, 16)
            for g in range(0, QG, 4):
                sp.dma_start(wqk_sb[:, :, g:g + 4], wqk[:, :, g:g + 4]).then_inc(s_wqk, 16)
            sp.dma_start(mask_f, masks).then_inc(s_const, 16)
            sp.dma_start(rowmask_sb[:], rowmask).then_inc(s_const, 16)
            sp.dma_start(x_res[:], load_x(0)).then_inc(s_xres, 16)
            sp.dma_start(ctx_sb[:], ctxT[0]).then_inc(s_ctx, 16)
            sp.dma_start(xwk_sb[:], xwk).then_inc(s_xw, 16)
            sp.dma_start(xwv_sb[:], xwv).then_inc(s_xw, 16)
            sp.dma_start(wo_sb[:], wo).then_inc(s_wo, 16)
            sp.dma_start(xwq_sb[:], xwq).then_inc(s_xw, 16)
            sp.dma_start(xwo_sb[:], xwo).then_inc(s_xw, 16)
            sp.dma_start(wgu_sb[:], wgu).then_inc(s_wgu, 16)
            sp.dma_start(wd_sb[:], wd).then_inc(s_wd, 16)

            for b in range(B):
                if b + 1 < B:
                    sp.wait_ge(s_xn, 3 * b - 1 if b else 1)
                    sp.dma_start(x_ln[:], load_x(b + 1)).then_inc(s_xln, 16)
                    wait_drained(sp, "wo", b)
                    sp.dma_start(x_res[:], load_x(b + 1)).then_inc(s_xres, 16)
                    wait_filled(sp, "v2", b)
                    sp.dma_start(ctx_sb[:], ctxT[b + 1]).then_inc(s_ctx, 16)
                wait_drained(sp, "down", b)
                sp.dma_start(out[b].rearrange("(t p) d -> p t d", p=P), y[:]).then_inc(s_out, 16)
            sp.wait_ge(s_out, 16 * B)

        @block.tensor
        def _(pe):
            def claim(name, b):
                k, n = ring_use(name, b)
                if not (isinstance(n, int) and n == 0):
                    pe.wait_ge(s_drained[k], n)

            def transpose_norm(name, b, which, n):
                claim(name, b)
                pe.wait_ge(s_xn, n)
                o = half_banks(name, b)
                for k in range(KT):
                    for t in range(TT):
                        mm = pe.transpose(o[:, k, t * P:(t + 1) * P], xn[:, which, t, k * P:(k + 1) * P],
                                          ident_sb[:])
                mm.then_inc(filled(name, b), 1)

            def rope_group(name, b, g):
                claim(name, b)
                o = half_banks(name, b)
                for half in range(2):
                    for k in range(KT):
                        mm = pe.matmul(o[:, half, :], wqk_sb[:, k, g, half, :], xnT[:, 0, k, :],
                                       start=(k == 0), stop=(k == KT - 1))
                mm.then_inc(filled(name, b), 1)

            def v_tile(name, b, t):
                claim(name, b)
                for k in range(KT):
                    mm = pe.matmul(bank(name, b), xnT[:, 0, k, t * P:(t + 1) * P], wv_sb[:, k, :],
                                   start=(k == 0), stop=(k == KT - 1))
                mm.then_inc(filled(name, b), 1)

            def unit_scores(b, i):
                u = UNITS * b + i
                if not (isinstance(b, int) and u < 2):
                    pe.wait_ge(s_sub, u - 1)
                o = ps[:, BANK_S + i % 2, :]
                if i < NQB:
                    if i == 0:
                        pe.wait_ge(s_addP, pool_sums(RG) * (b + 1))
                        pe.wait_ge(s_addV, RG * (b + 1))
                    pe.matmul(o, ident_bf[:], mask_sb[:, 0 if i == 0 else 1, :], start=True, stop=False,
                              skip_group_check=True)
                    for p in range(PAIRS):
                        mm = pe.matmul(o[:, p * P:(p + 1) * P], qs_rows[:, p, i * P:(i + 1) * P],
                                       kd[:, p, :, i * QB:i * QB + WK], start=False, stop=(p == PAIRS - 1),
                                       skip_group_check=True)
                else:
                    j = i - NQB
                    if j == 0:
                        wait_drained(pe, "q2", b)
                        pe.wait_ge(s_k2a, b + 1)
                    if j == XU0 // HG:
                        pe.wait_ge(s_k2p, b + 1)
                    tile = 0 if j < XU0 else 1
                    n = 4 if tile == 0 else 2
                    h0 = j * 4 if tile == 0 else (j - XU0) * 2
                    pe.matmul(o, ident_bf[:], mask_sb[:, 2 + tile, :], start=True, stop=False,
                              skip_group_check=True)
                    mm = pe.matmul(o, q2T[:, h0 // HPT, tile * P:(tile + 1) * P],
                                   k2d[:, h0 // HPT, h0 % HPT:h0 % HPT + n, 0:(tile + 1) * P],
                                   start=False, stop=True, skip_group_check=True)
                mm.then_inc(s_score, 1)

            def unit_transpose(b, i):
                u = UNITS * b + i
                pe.wait_ge(s_norm, u + 1)
                if not (isinstance(b, int) and u < 2):
                    pe.wait_ge(s_pT, u - 1)
                for c in range(4):
                    mm = pe.transpose(ps[:, BANK_PT + i % 2, c * P:(c + 1) * P],
                                      prob[:, i % ND, c * P:(c + 1) * P], ident_sb[:])
                mm.then_inc(s_tr, 1)

            def unit_values(b, i):
                u = UNITS * b + i
                pe.wait_ge(s_pT, u + 1)
                pT_i = pT[:, i % 2, :].rearrange("p (c n) -> p c n", c=4)
                if i < NQB:
                    if i == 0:
                        wait_before(pe, "v0", b)
                        wait_before(pe, "v1", b)
                        if not (isinstance(b, int) and b == 0):
                            pe.wait_ge(s_o2T, b)
                    else:
                        pe.wait_ge(s_oT, NQB * b + i)
                    for p in range(PAIRS):
                        mm = pe.matmul(ps[:, BANK_O, p * P:(p + 1) * P], vb[:, i, p, :], pT_i[:, p, :],
                                       start=True, stop=True)
                else:
                    j = i - NQB
                    if j == 0:
                        wait_drained(pe, "v2", b)
                        pe.wait_ge(s_oT, NQB * (b + 1))
                    tile = 0 if j < XU0 else 1
                    h0 = j * 4 if tile == 0 else (j - XU0) * 2
                    for pair in range(2 - tile):
                        quad = (h0 + 2 * pair) % HPT // 2
                        o = ps[32 * quad:32 * quad + 32, BANK_O, :].rearrange("p (g s) -> p g s", g=HG)
                        n = 0
                        for h in range(2):
                            for kt in range(tile + 1):
                                c = (2 * pair + h) if tile == 0 else 2 * h + kt
                                mm = pe.matmul(o[:, h0 // HPT, tile * P:(tile + 1) * P],
                                               v2z[:, kt, h0 + 2 * pair + h, :], pT_i[:, c, :],
                                               start=(n == 0), stop=(n == 2 * (tile + 1) - 1))
                                n += 1
                mm.then_inc(s_av, 1)

            def window_out(b, t):
                if t == 0:
                    claim("wo", b)
                pe.wait_ge(s_oT, NQB * b + NQB // TT * (t + 1))
                n = 0
                for p in range(PAIRS):
                    for r in range(R):
                        mm = pe.matmul(half_banks("wo", b)[:, t, :], qs[:, p, t * P:(t + 1) * P, r],
                                       wo_sb[:, p, r, :], start=(n == 0), stop=(n == H // 2 - 1))
                        n += 1
                if t == TT - 1:
                    mm.then_inc(filled("wo", b), 1)

            def latent_kv(b):
                pe.wait_ge(s_ctx, 16 * (b + 1))
                claim("k2", b)
                for g in range(HG):
                    mm = pe.matmul(half_banks("k2", b)[:, g, :], xwk_sb[:, g * P:(g + 1) * P], ctx_sb[:],
                                   start=True, stop=True)
                mm.then_inc(filled("k2", b), 1)
                claim("v2", b)
                for t in range(TT):
                    mm = pe.matmul(half_banks("v2", b)[:, t, :], ctx_sb[:, t * P:(t + 1) * P], xwv_sb[:],
                                   start=True, stop=True)
                mm.then_inc(filled("v2", b), 1)

            def cross_q(b):
                claim("q2", b)
                wait_drained(pe, "ln2", b)
                for g in range(HG):
                    for k in range(KT):
                        mm = pe.matmul(half_banks("q2", b)[:, g, :], xwq_sb[:, k, g * P:(g + 1) * P],
                                       xnT[:, 1, k, :], start=(k == 0), stop=(k == KT - 1))
                mm.then_inc(filled("q2", b), 1)

            def cross_out(b):
                claim("out", b)
                pe.wait_ge(s_o2T, b + 1)
                for t in range(TT):
                    for g in range(HG):
                        mm = pe.matmul(half_banks("out", b)[:, t, :], o2T[:, g, t * P:(t + 1) * P],
                                       xwo_sb[:, g, :], start=(g == 0), stop=(g == HG - 1))
                mm.then_inc(filled("out", b), 1)

            def gate_up(b, c, j):
                for w, name in enumerate(("gate", "up")):
                    use = f"{name}{c}{j}"
                    claim(use, b)
                    for m in range(2):
                        for k in range(KT):
                            mm = pe.matmul(half_banks(use, b)[:, m, :], wgu_sb[:, k, w, c * 4 + 2 * j + m, :],
                                           xnT[:, 2, k, :], start=(k == 0), stop=(k == KT - 1))
                    mm.then_inc(filled(use, b), 1)

            def down(b, c):
                if c == 0:
                    claim("down", b)
                pe.wait_ge(s_kept, FC * b + c + 1)
                for t in range(TT):
                    for j in range(4):
                        mm = pe.matmul(half_banks("down", b)[:, t, :], hidden[:, c, j, t * P:(t + 1) * P],
                                       wd_sb[:, c * 4 + j, :], start=(c == 0 and t == 0 and j == 0),
                                       stop=(c == FC - 1 and j == 3), skip_group_check=True)
                if c == FC - 1:
                    mm.then_inc(filled("down", b), 1)

            def batch(b, more):
                for i in range(NQB + LAG_V):
                    if i < NQB:
                        unit_scores(b, i)
                    if i == 3 and more:
                        transpose_norm("ln1", b, 0, 3 * (b + 1) + 1 - 2)
                    if i == NQB:
                        latent_kv(b)
                    if LAG_T <= i < NQB + LAG_T:
                        unit_transpose(b, i - LAG_T)
                    if i == NQB + 2:
                        window_out(b, 0)
                    if i >= LAG_V:
                        unit_values(b, i - LAG_V)
                window_out(b, 1)
                if more:
                    wait_drained(pe, "ln1", b)
                    rope_group("k0", b, QG)
                    rope_group("k1", b, QG + 1)
                    v_tile("v0", b, 0)
                transpose_norm("ln2", b, 1, 3 * b + (3 if more else 2))
                if more:
                    v_tile("v1", b, 1)
                cross_q(b)
                for i in range(XU + LAG_V):
                    if i < XU:
                        unit_scores(b, NQB + i)
                    if i >= XU and more:
                        rope_group(QNAME[i - XU], b, i - XU)
                    if LAG_T <= i < XU + LAG_T:
                        unit_transpose(b, NQB + i - LAG_T)
                    if i >= LAG_V:
                        unit_values(b, NQB + i - LAG_V)
                cross_out(b)
                if more:
                    for g in range(3, 6):
                        rope_group(QNAME[g], b, g)
                transpose_norm("ln3", b, 2, 3 * b + (4 if more else 3))
                if more:
                    for g in range(6, QG):
                        rope_group(QNAME[g], b, g)
                wait_drained(pe, "ln3", b)
                for c in range(FC):
                    for j in range(2):
                        gate_up(b, c, j)
                for c in range(FC):
                    down(b, c)

            pe.wait_ge(s_const, 16 * 4)
            transpose_norm("ln1", None, 0, 1)
            wait_drained(pe, "ln1", None)
            pe.wait_ge(s_wqk, 16 * (GROUPS + 2))
            rope_group("k0", None, QG)
            rope_group("k1", None, QG + 1)
            pe.wait_ge(s_wv, 16)
            v_tile("v0", None, 0)
            v_tile("v1", None, 1)
            for g in range(QG):
                rope_group(QNAME[g], None, g)
            pe.wait_ge(s_cbf, 2)
            pe.wait_ge(s_zero, 3)
            pe.wait_ge(s_wo, 16)
            pe.wait_ge(s_xw, 16 * 4)
            pe.wait_ge(s_wgu, 16)
            pe.wait_ge(s_wd, 16)
            for b in range(B):
                batch(b, b + 1 < B)

        @block.vector
        def _(dve):
            def layer_norm(src, which, n):
                for t in range(TT):
                    ins = dve.bn_stats(stats[:, which, t, :], src[:, t, :])
                ins.then_inc(s_stats, 1)
                dve.wait_ge(s_stats, n)
                for t in range(TT):
                    ins = dve.bn_aggr(moments[:, which, t, :], stats[:, which, t, :])
                ins.then_inc(s_mom, 1)
                dve.wait_ge(s_mom, n)
                dve.tensor_scalar(vareps[:, which, :], moments[:, which, :, 1], EPS, None,
                                  ALU.add).then_inc(s_var, 1)
                dve.wait_ge(s_rstd, n)
                for t in range(TT):
                    ins = dve.tensor_scalar(xn[:, which, t, :], src[:, t, :], moments[:, which, t, 0:1],
                                            rstd[:, which, t:t + 1], ALU.subtract, ALU.mult)
                ins.then_inc(s_xn, 1)

            def rope_group(name, b, g, n):
                wait_filled(dve, name, b)
                if n > 2:
                    dve.wait_ge(s_addP, pool_sums(n - 2))
                src = half_banks(name, b)
                ring = (n - 1) % 2
                cos, sin = rope[:, ring, 0], rope[:, ring, 1]
                dve.tensor_tensor(cos, src, trig_sb[:, 0:1, :].broadcast_to([P, 2, S]), ALU.mult)
                dve.tensor_tensor(sin, src, trig_sb[:, 1:3, :], ALU.mult)\
                   .then_inc(drained(name, b), 1)

            def rope_sums(name, b, g, n):
                wait_drained(dve, name, b)
                ring = (n - 1) % 2
                cos, sin = rope[:, ring, 0], rope[:, ring, 1]
                if g < QG:
                    G, r = g // R, g % R
                    for up in range(2):
                        rows = slice(64 * up, 64 * up + 64)
                        ins = dve.tensor_tensor(qs[64:128, 2 * G + up, :, r], cos[rows, 1, :], sin[rows, 0, :],
                                                ALU.add)
                else:
                    G = g - QG
                    for i in range(4):
                        rows = slice(32 * i, 32 * i + 32)
                        to = 64 + 32 * (i % 2)
                        ins = dve.tensor_tensor(kd[to:to + 32, 2 * G + i // 2, i % 2, WIN:], cos[rows, 1, :],
                                                sin[rows, 0, :], ALU.add)
                ins.then_inc(s_addV, 1)

            def unit_shape(i):
                return dict(g=8 if i < NQB else (4 if i - NQB < XU0 else 2))

            def unit_max(b, i):
                u = UNITS * b + i
                g = unit_shape(i)["g"]
                src = ps[:, BANK_S + i % 2, :].rearrange("p (g k) -> p g k", g=g)
                dve.wait_ge(s_score, u + 1)
                dve.tensor_reduce(mx[:, i % ND, 0:g], src, AX.X, ALU.max).then_inc(s_max, 1)
                dve.wait_ge(s_max, u + 1)
                if not (isinstance(b, int) and u < ND):
                    dve.wait_ge(s_tr, u - ND + 1)
                dve.tensor_tensor(prob[:, i % ND, :].rearrange("p (g k) -> p g k", g=g), src,
                                  mx[:, i % ND, 0:g].unsqueeze(2).broadcast_to([P, g, 512 // g]),
                                  ALU.subtract).then_inc(s_sub, 1)

            def unit_sum(b, i):
                u = UNITS * b + i
                g = unit_shape(i)["g"]
                dve.wait_ge(s_exp, u + 1)
                dve.tensor_reduce(total[:, i % ND, 0:g], prob[:, i % ND, :].rearrange("p (g k) -> p g k", g=g),
                                  AX.X, ALU.add).then_inc(s_sum, 1)
                dve.wait_ge(s_sum, u + 1)
                if not (isinstance(b, int) and u < ND):
                    dve.wait_ge(s_norm, u - ND + 1)
                dve.reciprocal(inv[:, i % ND, 0:g], total[:, i % ND, 0:g]).then_inc(s_inv, 1)

            def chunk_values(b, c, j):
                wait_filled(dve, f"up{c}{j}", b)
                wait_drained(dve, f"gate{c}{j}", b)
                h = hidden[:, c, 2 * j:2 * j + 2, :]
                dve.tensor_tensor(h, h, half_banks(f"up{c}{j}", b), ALU.mult)\
                   .then_inc(drained(f"up{c}{j}", b), 1)

            def sparsify(b, c):
                n = FC * b + c + 1
                dve.wait_ge(s_mag, n)
                dve.tensor_tensor(beats[:, 0:2, :], mag[:, 0::2, :], mag[:, 1::2, :], ALU.is_ge)
                dve.tensor_tensor(beats[:, 2:4, :], mag[:, 0:2, :], mag[:, 2:4, :], ALU.is_ge)
                dve.tensor_tensor(beats[:, 4, :], mag[:, 0, :], mag[:, 3, :], ALU.is_ge)
                dve.tensor_tensor(beats[:, 5, :], mag[:, 1, :], mag[:, 2, :], ALU.is_ge).then_inc(s_beats, 1)
                dve.wait_ge(s_beats, n)
                b01, b23, b02, b13, b03, b12 = (beats[:, k, :] for k in range(6))
                dve.tensor_tensor(part[:, 0:2, :], beats[:, 2:4, :], beats[:, 4:6, :], ALU.add)
                dve.tensor_tensor(part[:, 2, :], b02, b12, ALU.add)
                dve.tensor_tensor(part[:, 3, :], b13, b03, ALU.add).then_inc(s_part, 1)
                dve.wait_ge(s_part, n)
                dve.tensor_tensor(wins[:, 0, :], part[:, 0, :], b01, ALU.add)
                dve.tensor_tensor(wins[:, 1, :], part[:, 1, :], b01, ALU.subtract)
                dve.tensor_tensor(wins[:, 2, :], b23, part[:, 2, :], ALU.subtract)
                dve.tensor_tensor(wins[:, 3, :], part[:, 3, :], b23, ALU.add).then_inc(s_wins, 1)
                dve.wait_ge(s_wins, n)
                for j, (op, least) in enumerate(((ALU.is_ge, 2.0), (ALU.is_ge, 1.0), (ALU.is_ge, 0.0),
                                                 (ALU.is_le, 1.0))):
                    ins = dve.scalar_tensor_tensor(hidden[:, c, j, :], wins[:, j, :], least, hidden[:, c, j, :],
                                                   op, ALU.mult)
                ins.then_inc(s_kept, 1)

            def add_out(b):
                wait_filled(dve, "down", b)
                if not (isinstance(b, int) and b == 0):
                    dve.wait_ge(s_out, 16 * b)
                dve.tensor_tensor(y[:], half_banks("down", b), x2[:], ALU.add)\
                   .then_inc(drained("down", b), 1)

            def batch(b, more):
                for i in range(NQB + 1):
                    if i < NQB:
                        unit_max(b, i)
                    if i >= 1:
                        unit_sum(b, i - 1)
                    if i == 1 and more:
                        dve.wait_ge(s_xln, 16 * (b + 2))
                        layer_norm(x_ln, 0, 3 * b + 2)
                wait_filled(dve, "wo", b)
                dve.wait_ge(s_xres, 16 * (b + 1))
                dve.tensor_tensor(x1[:], half_banks("wo", b), x_res[:], ALU.add)\
                   .then_inc(drained("wo", b), 1)
                wait_drained(dve, "wo", b)
                layer_norm(x1, 1, 3 * b + (3 if more else 2))
                n = RG * (b + 1)
                if more:
                    for g in range(GROUPS):
                        rope_group(f"k{g}", b, QG + g, n + g + 1)
                        rope_sums(f"k{g}", b, QG + g, n + g + 1)
                for i in range(XU + 1):
                    if i < XU:
                        unit_max(b, NQB + i)
                    if i >= 1:
                        unit_sum(b, NQB + i - 1)
                if more:
                    for g in range(3):
                        rope_group(QNAME[g], b, g, n + GROUPS + g + 1)
                        rope_sums(QNAME[g], b, g, n + GROUPS + g + 1)
                wait_filled(dve, "out", b)
                dve.tensor_tensor(x2[:], half_banks("out", b), x1[:], ALU.add)\
                   .then_inc(drained("out", b), 1)
                wait_drained(dve, "out", b)
                layer_norm(x2, 2, 3 * b + (4 if more else 3))
                if more:
                    for g in range(3, QG):
                        rope_group(QNAME[g], b, g, n + GROUPS + g + 1)
                        rope_sums(QNAME[g], b, g, n + GROUPS + g + 1)
                for c in range(FC):
                    for j in range(2):
                        chunk_values(b, c, j)
                    sparsify(b, c)
                add_out(b)

            dve.memset(power[:], -0.5).then_inc(s_zero, 1)
            dve.wait_ge(s_xln, 16)
            layer_norm(x_ln, 0, 1)
            dve.memset(v2z[:], 0.0).then_inc(s_zero, 1)
            dve.wait_ge(s_const, 16 * 4)
            dve.tensor_copy(ident_bf[:], ident_sb[:]).then_inc(s_cbf, 1)
            dve.wait_ge(s_zero, 3)
            for g in range(GROUPS):
                rope_group(f"k{g}", None, QG + g, g + 1)
                rope_sums(f"k{g}", None, QG + g, g + 1)
            dve.tensor_copy(mask_sb[:], mask_f).then_inc(s_cbf, 1)
            for g in range(QG):
                rope_group(QNAME[g], None, g, GROUPS + g + 1)
                rope_sums(QNAME[g], None, g, GROUPS + g + 1)
            for b in range(B):
                batch(b, b + 1 < B)

        @block.gpsimd
        def _(pool):
            def inverse_root(which, n):
                pool.wait_ge(s_var, n)
                pool.tensor_tensor(rstd[:, which, :], vareps[:, which, :], power[:], ALU.pow).then_inc(s_rstd, 1)

            def rope_sums(name, b, g, n):
                wait_drained(pool, name, b)
                ring = (n - 1) % 2
                cos, sin = rope[:, ring, 0], rope[:, ring, 1]
                done = pool_sums(n - 1)
                if g < QG:
                    G, r = g // R, g % R
                    for up in range(2):
                        if done + up:
                            pool.wait_ge(s_addP, done + up)
                        rows = slice(64 * up, 64 * up + 64)
                        pool.tensor_tensor(qs[0:64, 2 * G + up, :, r], cos[rows, 0, :], sin[rows, 1, :],
                                           ALU.add).then_inc(s_addP, 1)
                else:
                    G = g - QG
                    for i in range(4):
                        if done + i:
                            pool.wait_ge(s_addP, done + i)
                        rows = slice(32 * i, 32 * i + 32)
                        to = 32 * (i % 2)
                        pool.tensor_tensor(kd[to:to + 32, 2 * G + i // 2, i % 2, WIN:], cos[rows, 0, :],
                                           sin[rows, 1, :], ALU.add).then_inc(s_addP, 1)

            def unit_norm(b, i):
                u = UNITS * b + i
                g = 8 if i < NQB else (4 if i - NQB < XU0 else 2)
                pool.wait_ge(s_inv, u + 1)
                p = prob[:, i % ND, :].rearrange("p (g k) -> p g k", g=g)
                pool.tensor_tensor(p, p, inv[:, i % ND, 0:g].unsqueeze(2).broadcast_to([P, g, 512 // g]),
                                   ALU.mult).then_inc(s_norm, 1)

            def batch(b, more):
                pool.wait_ge(s_addP, pool_sums(RG) * (b + 1))
                for i in range(NQB):
                    if i == 1 and more:
                        inverse_root(0, 3 * b + 2)
                    unit_norm(b, i)
                inverse_root(1, 3 * b + (3 if more else 2))
                wait_drained(pool, "k2", b)
                for h in range(HPT):
                    ins = pool.tensor_scalar(k2d[:, 1, h, :], k2T[:, 1, :], rowmask_sb[:, h:h + 1], None, ALU.mult)
                ins.then_inc(s_k2p, 1)
                n = RG * (b + 1)
                if more:
                    pool.wait_ge(s_k2p, b + 1)
                    for g in range(GROUPS):
                        rope_sums(f"k{g}", b, QG + g, n + g + 1)
                    pool.wait_ge(s_addP, pool_sums(RG) * (b + 1) + pool_sums(GROUPS))
                for i in range(XU):
                    unit_norm(b, NQB + i)
                if more:
                    pool.wait_ge(s_norm, UNITS * (b + 1))
                    for g in range(3):
                        rope_sums(QNAME[g], b, g, n + GROUPS + g + 1)
                    pool.wait_ge(s_addP, pool_sums(RG) * (b + 1) + pool_sums(GROUPS + 3))
                inverse_root(2, 3 * b + (4 if more else 3))
                if more:
                    pool.wait_ge(s_rstd, 3 * b + 4)
                    for g in range(3, QG):
                        rope_sums(QNAME[g], b, g, n + GROUPS + g + 1)

            pool.wait_ge(s_zero, 1)
            inverse_root(0, 1)
            pool.memset(kd[:], 0.0)
            pool.memset(vb[:], 0.0).then_inc(s_zero, 1)
            pool.wait_ge(s_zero, 3)
            pool.wait_ge(s_const, 16 * 4)
            for g in range(GROUPS):
                rope_sums(f"k{g}", None, QG + g, g + 1)
            for g in range(QG):
                rope_sums(QNAME[g], None, g, GROUPS + g + 1)
            for b in range(B):
                batch(b, b + 1 < B)

        @block.scalar
        def _(act):
            def copy_norm(name, b, which):
                wait_filled(act, name, b)
                act.activation(xnT[:, which], half_banks(name, b), ACT.Copy)\
                   .then_inc(drained(name, b), 1)

            def v_blocks(name, b, t):
                wait_filled(act, name, b)
                src = bank(name, b).rearrange("p (c e d) -> p c e d", c=PAIRS, e=2)
                for q in range(P // QB):
                    u = P // QB * t + q
                    for e in range(2):
                        for own in range(2):
                            if u + 1 - own >= NQB:
                                continue
                            to = 64 * e + WIN * own
                            ins = act.activation(vb[to:to + QB, u + 1 - own, :, e * HD:(e + 1) * HD],
                                                 src[q * QB:(q + 1) * QB, :, e, :], ACT.Copy)
                ins.then_inc(drained(name, b), 1)

            def unit_exp(b, i):
                u = UNITS * b + i
                act.wait_ge(s_sub, u + 1)
                p = prob[:, i % ND, :]
                act.activation(p, p, ACT.Exp, scale=float((HD if i < NQB else XD) ** -0.5)).then_inc(s_exp, 1)

            def unit_pT(b, i):
                u = UNITS * b + i
                act.wait_ge(s_tr, u + 1)
                if not (isinstance(b, int) and u < 2):
                    act.wait_ge(s_av, u - 1)
                act.activation(pT[:, i % 2, :], ps[:, BANK_PT + i % 2, :], ACT.Copy).then_inc(s_pT, 1)

            def unit_out(b, i):
                act.wait_ge(s_av, UNITS * b + i + 1)
                act.activation(qs_rows[:, :, i * P:(i + 1) * P],
                               ps[:, BANK_O, :].rearrange("p (c n) -> p c n", c=PAIRS), ACT.Copy).then_inc(s_oT, 1)

            def latent_kv(b):
                wait_filled(act, "k2", b)
                act.activation(k2T[:], half_banks("k2", b), ACT.Copy)\
                   .then_inc(drained("k2", b), 1)
                wait_filled(act, "v2", b)
                src = half_banks("v2", b).rearrange("p t (h e d) -> p t h e d", h=XH // 2, e=2)
                for e in range(2):
                    for t in range(TT):
                        ins = act.activation(v2z[:, t, e::2, e * XD:(e + 1) * XD], src[:, t, :, e, :], ACT.Copy)
                ins.then_inc(drained("v2", b), 1)

            def batch(b, more):
                for i in range(NQB + LAG_V):
                    if i < NQB:
                        unit_exp(b, i)
                    if i == 3 and more:
                        copy_norm("ln1", b, 0)
                    if LAG_T <= i < NQB + LAG_T:
                        unit_pT(b, i - LAG_T)
                    if i >= LAG_V:
                        unit_out(b, i - LAG_V)
                    if i == NQB:
                        latent_kv(b)
                wait_drained(act, "k2", b)
                for h in range(HPT):
                    ins = act.activation(k2d[:, 0, h, :], k2T[:, 0, :], ACT.Copy, scale=rowmask_sb[:, h:h + 1])
                ins.then_inc(s_k2a, 1)
                if more:
                    v_blocks("v0", b, 0)
                copy_norm("ln2", b, 1)
                if more:
                    v_blocks("v1", b, 1)
                wait_filled(act, "q2", b)
                act.activation(q2T[:], half_banks("q2", b), ACT.Copy)\
                   .then_inc(drained("q2", b), 1)
                for i in range(XU + LAG_T):
                    if i < XU:
                        unit_exp(b, NQB + i)
                    if i >= LAG_T:
                        unit_pT(b, NQB + i - LAG_T)
                act.wait_ge(s_av, UNITS * (b + 1))
                act.activation(o2T[:], ps[:, BANK_O, :].rearrange("p (g s) -> p g s", g=HG), ACT.Copy)\
                   .then_inc(s_o2T, 1)
                copy_norm("ln3", b, 2)
                for c in range(FC):
                    for j in range(2):
                        use = f"gate{c}{j}"
                        wait_filled(act, use, b)
                        if not (isinstance(b, int) and b == 0):
                            wait_filled(act, "down", b - 1)
                        act.activation(hidden[:, c, 2 * j:2 * j + 2, :], half_banks(use, b), ACT.Silu)\
                   .then_inc(drained(use, b), 1)
                    wait_drained(act, f"up{c}1", b)
                    if c or not (isinstance(b, int) and b == 0):
                        act.wait_ge(s_beats, FC * b + c)
                    act.activation(mag[:], hidden[:, c], ACT.Abs).then_inc(s_mag, 1)

            act.wait_ge(s_const, 16 * 4)
            copy_norm("ln1", None, 0)
            act.wait_ge(s_zero, 3)
            v_blocks("v0", None, 0)
            v_blocks("v1", None, 1)
            for b in range(B):
                batch(b, b + 1 < B)


def constants():
    inv_freq = (1.0 / np.float32(10000.0) ** (np.arange(0, HD, 2, dtype=np.float32) / np.float32(HD)))
    angle = np.arange(S, dtype=np.float32)[:, None] * inv_freq.astype(np.float32)[None, :]
    cos, sin = np.cos(angle).T, np.sin(angle).T
    trig = np.tile(np.stack([cos, sin, -sin], axis=1), (4, 1, 1)).astype(np.float32)
    q, k = np.arange(QB)[:, None], np.arange(WK)[None, :]
    hidden = (k > WIN + q) | (k < q)
    first = hidden | (k < WIN)
    masks = np.zeros((P, 4, 512), np.float32)
    masks[:, 0] = np.tile(np.repeat(np.where(first, MASKED, 0.0), R, 0), (1, KV))
    masks[:, 1] = np.tile(np.repeat(np.where(hidden, MASKED, 0.0), R, 0), (1, KV))
    later = np.where(np.arange(P)[None, :] > np.arange(P)[:, None], MASKED, 0.0)
    masks[:, 2] = np.tile(later, (1, 4))
    masks[:, 3] = np.tile(np.concatenate([np.zeros((P, P)), later], 1), (1, 2))
    rowmask = (np.arange(P)[:, None] // XD == np.arange(HPT)[None, :]).astype(np.float32)
    return trig, masks, np.eye(P, dtype=np.float32), rowmask


def kernel(x, ctx_512, L0_attn_wq, L0_attn_wk, L0_attn_wv, L0_attn_wo, L0_xattn_Wq, L0_xattn_Wkv_expand,
           L0_xattn_Wout, L0_ffn_w_gate, L0_ffn_w_up, L0_ffn_w_down):
    import concourse.bacc as bacc
    from concourse.bass_utils import run_bass_kernel_spmd

    a = np.asarray
    q = a(L0_attn_wq).reshape(GROUPS, 4, R, 2, HALF, D).transpose(5, 0, 2, 3, 1, 4).reshape(D, QG, 2, P)
    k = a(L0_attn_wk).reshape(GROUPS, 4, 2, HALF, D).transpose(4, 0, 2, 1, 3).reshape(D, GROUPS, 2, P)
    by_k = lambda w: w.reshape(KT, P, *w.shape[1:]).swapaxes(0, 1)
    ffn = lambda w: by_k(a(w).reshape(D, FC, P, 4).transpose(0, 1, 3, 2).reshape(D, FC * 4, P))
    trig, masks, ident, rowmask = constants()
    arrays = {
        "x": a(x),
        "ctxT": a(ctx_512)[:, :S].transpose(0, 2, 1),
        "wqk": by_k(np.concatenate([q, k], axis=1)),
        "wv": by_k(a(L0_attn_wv).T),
        "wo": a(L0_attn_wo).T.reshape(PAIRS, 2, R, HD, D).transpose(1, 3, 0, 2, 4).reshape(P, PAIRS, R, D),
        "xwq": by_k(a(L0_xattn_Wq).T),
        "xwk": a(L0_xattn_Wkv_expand)[:D].T,
        "xwv": a(L0_xattn_Wkv_expand)[D:].T,
        "xwo": by_k(a(L0_xattn_Wout).T),
        "wgu": np.stack([ffn(L0_ffn_w_gate), ffn(L0_ffn_w_up)], axis=2),
        "wd": a(L0_ffn_w_down).reshape(FC, P, 4, D).transpose(1, 0, 2, 3).reshape(P, FC * 4, D),
        "trig": trig, "masks": masks, "ident": ident, "rowmask": rowmask,
    }
    nc = bacc.Bacc("TRN2", target_bir_lowering=False, num_devices=1)
    args, feeds = {}, {}
    for name, v in arrays.items():
        feeds[f"in_{name}"] = np.ascontiguousarray(v)
        args[name] = nc.dram_tensor(f"in_{name}", v.shape, F32, kind="ExternalInput").ap()
    args["out"] = nc.dram_tensor("out_0", (B, S, D), F32, kind="ExternalOutput").ap()
    build(nc, **args)
    r = run_bass_kernel_spmd(nc, [feeds], core_ids=[0])
    return r.results[0]["out_0"]
```

```python
from contextlib import ExitStack

import numpy as np

import concourse.bass as bass
from concourse import mybir

ALU = mybir.AluOpType
ACT = mybir.ActivationFunctionType
AX = mybir.AxisListType
F32 = mybir.dt.float32
F32R = mybir.dt.float32r
BF16 = mybir.dt.bfloat16

P = 128
B, S, D = 4, 256, 256
KT = D // P
TT = S // P
H, KV, HD = 32, 8, 64
R = H // KV
HALF = HD // 2
WIN = 32
QB = 32
NQB = S // QB
WK = QB + WIN
PAIRS = KV // 2
GROUPS = KV // 4
QG = GROUPS * R
RG = QG + GROUPS
XH, XD, L = 16, 16, 64
HG = XH * XD // P
HPT = P // XD
XU0, XU1 = 4, 8
XU = XU0 + XU1
WCHUNKS = 8
RAW = 4
UNITS = NQB + XU
FF = 1024
FC = FF // (4 * P)
EPS = 1e-5
MASKED = -1.0e37
LAG_T, LAG_V = 3, 4
LN1_AT = 4
ND = 4
HEAD = 3
X_FILL = {2: 3, 13: 4}

BANK_S, BANK_PT, BANK_O, BANK_M = 0, 2, 4, 5
NM = 3
NF = 3

NEXT_USES = ["ln1", "k0", "k1", "v0", "q0", "q1", "q2", "q3", "q4", "v1", "q5", "q6", "q7", "xk", "xv"]
USES = ["ln1", "k0", "k1", "wo0", "v0", "wo1", "v1", "q0", "ln2", "q1", "xq", "q2", "q3", "q4", "q5",
        "out0", "out1", "q6", "q7", "ln3", "xk", "xv", "down"]
FFN_USES = [f"{w}{c}{j}" for c in range(FC) for j in range(2) for w in ("gate", "up")]
ORDER = [(u, None) for u in NEXT_USES] + [(u, b) for b in range(B) for u in USES
                                          if b + 1 < B or u not in NEXT_USES]
FFN_ORDER = [(u, b) for b in range(B) for u in FFN_USES]


def ring_use(name, b):
    if name in FFN_USES:
        n = FFN_ORDER.index((name, b))
        return NM + n % NF, n // NF
    n = ORDER.index((name, b))
    return n % NM, n // NM


def pool_sums(n):
    batches, m = divmod(n, RG)
    return batches * (4 * GROUPS + 2 * QG) + (4 * m if m <= GROUPS else 4 * GROUPS + 2 * (m - GROUPS))


def build(nc, x, ctxT, wqk, wv, wo, xwq, xwk, xwv, xwo, wgu, wd, trig, masks, ident, rowmask, out):
    es = ExitStack()
    with es:
        def sb(name, shape, dt=F32):
            return es.enter_context(nc.sbuf_tensor(name, shape, dt))

        def sem(name):
            return es.enter_context(nc.semaphore(name))

        wqk_sb = sb("wqk_sb", [P, KT, RG, 2, P])
        wv_sb = sb("wv_sb", [P, KT, KV * HD])
        wo_sb = sb("wo_sb", [P, PAIRS, R, D])
        xwq_sb = sb("xwq_sb", [P, KT, D])
        xwk_sb = sb("xwk_sb", [L, D])
        xwv_sb = sb("xwv_sb", [L, D])
        xwo_sb = sb("xwo_sb", [P, HG, D])
        wgu_hi = sb("wgu_hi", [P, KT, 2, FC * 4, P], F32R)
        wgu_lo = sb("wgu_lo", [P, KT, 2, FC * 4, P], F32R)
        wd_sb = sb("wd_sb", [P, FC * 4, D])
        trig_sb = sb("trig_sb", [P, 2, S])
        mask_sb = sb("mask_sb", [P, 2 * WK + P], BF16)
        mask_f = sb("mask_f", [P, 2 * WK + P])
        ident_sb = sb("ident_sb", [P, P])
        ident_bf = sb("ident_bf", [P, P], BF16)
        rowmask_sb = sb("rowmask_sb", [P, HPT])
        wcols = KT * 2 * FC * 4 * P // WCHUNKS
        raw = sb("raw", [P, RAW, wcols])
        x_ln = sb("x_ln", [P, TT, D])
        x_res = sb("x_res", [P, TT, D])
        stats = sb("stats", [P, 3, TT, 6])
        moments = sb("moments", [P, 3, TT, 2])
        vareps = sb("vareps", [P, 3, TT])
        power = sb("power", [P, TT])
        rstd = sb("rstd", [P, 3, TT])
        xn = sb("xn", [P, TT, D])
        xnT = sb("xnT", [P, 2, KT, S])
        x3_hi = sb("x3_hi", [P, KT, S], F32R)
        x3_lo = sb("x3_lo", [P, KT, S], F32R)
        rope = sb("rope", [P, 2, 2, 2, S])
        qs = sb("qs", [P, PAIRS, S, R])
        qs_rows = qs[:].rearrange("p c s r -> p c (s r)")
        kd = sb("kd", [P, PAIRS, 2, WIN + S])
        v_sb = sb("v_sb", [P, TT, KV * HD])
        vb = sb("vb", [P, NQB, PAIRS, 2 * HD])
        prob = sb("prob", [P, ND, 512])
        mx = sb("mx", [P, ND, 8])
        total = sb("total", [P, ND, 8])
        inv = sb("inv", [P, ND, 8])
        pT = sb("pT", [P, 2, 512])
        ctx_sb = sb("ctx_sb", [L, S])
        k2T = sb("k2T", [P, HG, S])
        k2d = sb("k2d", [P, HG, HPT, S])
        v2z = sb("v2z", [P, TT, XH, 2 * XD])
        q2T = sb("q2T", [P, HG, S])
        o2T = q2T
        work = k2d[:].rearrange("p g h s -> p (g h) s")
        hidden = work[:, 0:4 * FC, :].rearrange("p (c j) s -> p c j s", c=FC)
        mag = work[:, 4 * FC:4 * FC + 4, :]
        beats = work[:, 4 * FC + 4:4 * FC + 7, :].bitcast(BF16).rearrange("p a (b s) -> p (a b) s", b=2)
        part = sb("part", [P, 4, S], BF16)
        wins = sb("wins", [P, 4, S], BF16)

        ps = es.enter_context(nc.psum_tensor("ps", [P, 8, 512], F32))

        s_ident = sem("s_ident")
        s_trig = sem("s_trig")
        s_masks = sem("s_masks")
        s_wk = sem("s_wk")
        s_wq = [sem(f"s_wq{k}") for k in range(QG // 2)]
        s_wv = sem("s_wv")
        s_wrest = [sem(f"s_w{n}") for n in ("wo", "xattn", "d")]
        s_wo, s_xw, s_wd = s_wrest
        s_xkv = sem("s_xkv")
        s_xln = sem("s_xln")
        s_xres = sem("s_xres")
        s_ctx = sem("s_ctx")
        s_zero = sem("s_zero")
        s_cbf = sem("s_cbf")
        s_filled = [sem(f"s_filled{k}") for k in range(NM + NF)]
        s_drained = [sem(f"s_drained{k}") for k in range(NM + NF)]
        s_stats = sem("s_stats")
        s_mom = sem("s_mom")
        s_power = sem("s_power")
        s_var = sem("s_var")
        s_rstd = sem("s_rstd")
        s_xn = sem("s_xn")
        s_addP = sem("s_addP")
        s_addV = sem("s_addV")
        s_vb = sem("s_vb")
        s_x3hi = sem("s_x3hi")
        s_wraw = [sem(f"s_wraw{k}") for k in range(RAW)]
        s_whi = sem("s_whi")
        s_wlo = sem("s_wlo")
        s_score = sem("s_score")
        s_max = sem("s_max")
        s_sub = sem("s_sub")
        s_exp = sem("s_exp")
        s_sum = sem("s_sum")
        s_inv = sem("s_inv")
        s_norm = sem("s_norm")
        s_tr = sem("s_tr")
        s_pT = sem("s_pT")
        s_av = sem("s_av")
        s_oT = sem("s_oT")
        s_k2a = sem("s_k2a")
        s_k2v = sem("s_k2v")
        s_o2T = sem("s_o2T")
        s_mag = sem("s_mag")
        s_beats = sem("s_beats")
        s_part = sem("s_part")
        s_wins = sem("s_wins")
        s_kept = sem("s_kept")
        s_out = sem("s_out")

        def bank(name, b):
            k, _ = ring_use(name, b)
            return ps[:, BANK_M + k if k < NM else BANK_PT + k - NM, :]

        def half_banks(name, b):
            return bank(name, b).rearrange("p (t n) -> p t n", t=2)

        def wait_filled(eng, name, b):
            k, n = ring_use(name, b)
            eng.wait_ge(s_filled[k], n + 1)

        def wait_drained(eng, name, b):
            k, n = ring_use(name, b)
            eng.wait_ge(s_drained[k], n + 1)

        def before(b):
            return b - 1 if b else None

        def filled(name, b):
            return s_filled[ring_use(name, b)[0]]

        def drained(name, b):
            return s_drained[ring_use(name, b)[0]]

        flat = lambda w: w.rearrange("p k w c n -> p (k w c n)")
        wgu_c = [flat(wgu)[:, c * wcols:(c + 1) * wcols] for c in range(WCHUNKS)]
        hi_c = [flat(wgu_hi[:])[:, c * wcols:(c + 1) * wcols] for c in range(WCHUNKS)]
        lo_c = [flat(wgu_lo[:])[:, c * wcols:(c + 1) * wcols] for c in range(WCHUNKS)]

        def v_blocks(eng, copy, b, q):
            if q % (P // QB) == 0:
                wait_drained(eng, f"v{q // (P // QB)}", b)
            rows = slice(q % (P // QB) * QB, q % (P // QB) * QB + QB)
            src = v_sb[rows, q // (P // QB), :].rearrange("p (c e d) -> p c e d", c=PAIRS, e=2)
            for e in range(2):
                for own in range(2 if q + 1 < NQB else 1):
                    u = q + own
                    to = 64 * e + WIN * (1 - own)
                    ins = copy(vb[to:to + QB, u, :, e * HD:(e + 1) * HD], src[:, :, e, :])
            if q == NQB - 1:
                ins.then_inc(s_vb, 1)

        block = es.enter_context(nc.Block())

        @block.sync
        def _(sp):
            def load_x(b):
                return x[b].rearrange("(t p) d -> p t d", p=P)

            sp.dma_start(x_ln[:], load_x(0)).then_inc(s_xln, 16)
            sp.dma_start(ident_sb[:], ident).then_inc(s_ident, 16)
            for g in (QG, QG + 1):
                sp.dma_start(wqk_sb[:, :, g], wqk[:, :, g]).then_inc(s_wk, 16)
            sp.dma_start(trig_sb[:], trig).then_inc(s_trig, 16)
            sp.dma_start(wv_sb[:], wv).then_inc(s_wv, 16)
            for g in range(0, QG, 2):
                sp.dma_start(wqk_sb[:, :, g:g + 2], wqk[:, :, g:g + 2]).then_inc(s_wq[g // 2], 16)
            sp.dma_start(mask_f[:], masks).then_inc(s_masks, 16)
            sp.dma_start(rowmask_sb[:], rowmask).then_inc(s_masks, 16)
            sp.dma_start(xwk_sb[:], xwk).then_inc(s_xkv, 16)
            sp.dma_start(xwv_sb[:], xwv).then_inc(s_xkv, 16)
            sp.dma_start(ctx_sb[:], ctxT[0]).then_inc(s_ctx, 16)
            sp.dma_start(x_res[:], load_x(0)).then_inc(s_xres, 16)
            sp.dma_start(wo_sb[:], wo).then_inc(s_wo, 16)
            sp.dma_start(xwq_sb[:], xwq).then_inc(s_xw, 16)
            sp.dma_start(xwo_sb[:], xwo).then_inc(s_xw, 16)
            for c in range(RAW):
                sp.dma_start(raw[:, c, :], wgu_c[c]).then_inc(s_wraw[c], 16)
            sp.dma_start(wd_sb[:], wd).then_inc(s_wd, 16)

            sp.wait_ge(s_xn, TT)
            sp.dma_start(x_ln[:], load_x(1)).then_inc(s_xln, 16)
            wait_filled(sp, "xv", None)
            sp.dma_start(ctx_sb[:], ctxT[1]).then_inc(s_ctx, 16)
            for b in range(B):
                if b + 2 < B:
                    sp.wait_ge(s_xn, TT * (3 * b + 2))
                    sp.dma_start(x_ln[:], load_x(b + 2)).then_inc(s_xln, 16)
                if b == 0:
                    for c in range(RAW, WCHUNKS):
                        sp.wait_ge(s_wlo, c - RAW + 1)
                        sp.dma_start(raw[:, c % RAW, :], wgu_c[c]).then_inc(s_wraw[c % RAW], 16)
                if b + 2 < B:
                    wait_filled(sp, "xv", b)
                    sp.dma_start(ctx_sb[:], ctxT[b + 2]).then_inc(s_ctx, 16)
                wait_drained(sp, "down", b)
                sp.dma_start(out[b].rearrange("(t p) d -> p t d", p=P), x_res[:]).then_inc(s_out, 16)
                if b + 1 < B:
                    sp.wait_ge(s_out, 16 * (b + 1))
                    sp.dma_start(x_res[:], load_x(b + 1)).then_inc(s_xres, 16)
            sp.wait_ge(s_out, 16 * B)

        @block.tensor
        def _(pe):
            def claim(name, b):
                k, n = ring_use(name, b)
                if n:
                    pe.wait_ge(s_drained[k], n)

            def transpose_norm(name, b, n):
                claim(name, b)
                o = half_banks(name, b)
                for t in range(TT):
                    pe.wait_ge(s_xn, TT * (n - 1) + t + 1)
                    for k in range(KT):
                        mm = pe.transpose(o[:, k, t * P:(t + 1) * P], xn[:, t, k * P:(k + 1) * P],
                                          ident_sb[:])
                mm.then_inc(filled(name, b), 1)

            def rope_group(name, b, g, halves=(0, 1)):
                if 0 in halves:
                    claim(name, b)
                o = half_banks(name, b)
                for half in halves:
                    for k in range(KT):
                        mm = pe.matmul(o[:, half, :], wqk_sb[:, k, g, half, :], xnT[:, 0, k, :],
                                       start=(k == 0), stop=(k == KT - 1))
                if 1 in halves:
                    mm.then_inc(filled(name, b), 1)

            def v_tile(name, b, t):
                claim(name, b)
                for k in range(KT):
                    mm = pe.matmul(bank(name, b), xnT[:, 0, k, t * P:(t + 1) * P], wv_sb[:, k, :],
                                   start=(k == 0), stop=(k == KT - 1))
                mm.then_inc(filled(name, b), 1)

            def unit_scores(b, i):
                u = UNITS * b + i
                if u >= 2:
                    if i < 2:
                        pe.wait_ge(s_exp, u - 1)
                    elif i < NQB + 2:
                        pe.wait_ge(s_sub, NQB * b + i - 1)
                    else:
                        pe.wait_ge(s_exp, u - 1)
                o = ps[:, BANK_S + i % 2, :]
                if i < NQB:
                    if i == 0:
                        pe.wait_ge(s_addP, pool_sums(RG) * (b + 1))
                        pe.wait_ge(s_addV, RG * (b + 1))
                    at = 0 if i == 0 else WK
                    pe.matmul(o, ident_bf[:], mask_sb[:, at:at + WK].unsqueeze(1).broadcast_to([P, KV, WK]),
                              start=True, stop=False, skip_group_check=True)
                    for p in range(PAIRS):
                        mm = pe.matmul(o[:, p * P:(p + 1) * P], qs_rows[:, p, i * P:(i + 1) * P],
                                       kd[:, p, :, i * QB:i * QB + WK], start=False, stop=(p == PAIRS - 1),
                                       skip_group_check=True)
                else:
                    j = i - NQB
                    if j == 0:
                        wait_drained(pe, "xq", b)
                        pe.wait_ge(s_k2a, b + 1)
                    if j == XU0 // HG:
                        pe.wait_ge(s_k2v, b + 1)
                    tile = 0 if j < XU0 else 1
                    n = 4 if tile == 0 else 2
                    h0 = j * 4 if tile == 0 else (j - XU0) * 2
                    pe.matmul(o.rearrange("p (g k) -> p g k", g=n)[:, :, tile * P:(tile + 1) * P], ident_bf[:],
                              mask_sb[:, 2 * WK:].unsqueeze(1).broadcast_to([P, n, P]), start=True, stop=False,
                              skip_group_check=True)
                    mm = pe.matmul(o, q2T[:, h0 // HPT, tile * P:(tile + 1) * P],
                                   k2d[:, h0 // HPT, h0 % HPT:h0 % HPT + n, 0:(tile + 1) * P],
                                   start=False, stop=True, skip_group_check=True)
                mm.then_inc(s_score, 1)

            def ffn_banks_free(b):
                for use in FFN_USES[-NF:]:
                    wait_drained(pe, use, b - 1)

            def unit_transpose(b, i):
                u = UNITS * b + i
                pe.wait_ge(s_norm, u + 1)
                if b and i < 2:
                    ffn_banks_free(b)
                if u >= 2:
                    pe.wait_ge(s_pT, u - 1)
                for c in range(4):
                    mm = pe.transpose(ps[:, BANK_PT + i % 2, c * P:(c + 1) * P],
                                      prob[:, i % ND, c * P:(c + 1) * P], ident_sb[:])
                mm.then_inc(s_tr, 1)

            def unit_values(b, i):
                u = UNITS * b + i
                pe.wait_ge(s_pT, u + 1)
                pT_i = pT[:, i % 2, :].rearrange("p (c n) -> p c n", c=4)
                if i < NQB:
                    if i == 0:
                        pe.wait_ge(s_vb, b + 1)
                        if b:
                            pe.wait_ge(s_o2T, b)
                    else:
                        pe.wait_ge(s_oT, NQB * b + i)
                    for p in range(PAIRS):
                        mm = pe.matmul(ps[:, BANK_O, p * P:(p + 1) * P], vb[:, i, p, :], pT_i[:, p, :],
                                       start=True, stop=True)
                else:
                    j = i - NQB
                    if j == 0:
                        wait_drained(pe, "xv", before(b))
                        pe.wait_ge(s_oT, NQB * (b + 1))
                    tile = 0 if j < XU0 else 1
                    h0 = j * 4 if tile == 0 else (j - XU0) * 2
                    for pair in range(2 - tile):
                        quad = (h0 + 2 * pair) % HPT // 2
                        o = ps[32 * quad:32 * quad + 32, BANK_O, :].rearrange("p (g s) -> p g s", g=HG)
                        n = 0
                        for h in range(2):
                            for kt in range(tile + 1):
                                c = (2 * pair + h) if tile == 0 else 2 * h + kt
                                mm = pe.matmul(o[:, h0 // HPT, tile * P:(tile + 1) * P],
                                               v2z[:, kt, h0 + 2 * pair + h, :], pT_i[:, c, :],
                                               start=(n == 0), stop=(n == 2 * (tile + 1) - 1))
                                n += 1
                mm.then_inc(s_av, 1)

            def window_out(b, t):
                claim(f"wo{t}", b)
                pe.wait_ge(s_oT, NQB * b + NQB // TT * (t + 1))
                n = 0
                for p in range(PAIRS):
                    for r in range(R):
                        mm = pe.matmul(half_banks(f"wo{t}", b)[:, 0, :], qs[:, p, t * P:(t + 1) * P, r],
                                       wo_sb[:, p, r, :], start=(n == 0), stop=(n == H // 2 - 1))
                        n += 1
                mm.then_inc(filled(f"wo{t}", b), 1)

            def latent_kv(b, n):
                pe.wait_ge(s_ctx, 16 * n)
                claim("xk", b)
                for g in range(HG):
                    mm = pe.matmul(half_banks("xk", b)[:, g, :], xwk_sb[:, g * P:(g + 1) * P], ctx_sb[:],
                                   start=True, stop=True)
                mm.then_inc(filled("xk", b), 1)
                claim("xv", b)
                for t in range(TT):
                    mm = pe.matmul(half_banks("xv", b)[:, t, :], ctx_sb[:, t * P:(t + 1) * P], xwv_sb[:],
                                   start=True, stop=True)
                mm.then_inc(filled("xv", b), 1)

            def cross_q(b):
                claim("xq", b)
                wait_drained(pe, "ln2", b)
                for g in range(HG):
                    for k in range(KT):
                        mm = pe.matmul(half_banks("xq", b)[:, g, :], xwq_sb[:, k, g * P:(g + 1) * P],
                                       xnT[:, 1, k, :], start=(k == 0), stop=(k == KT - 1))
                mm.then_inc(filled("xq", b), 1)

            def cross_out(b):
                pe.wait_ge(s_o2T, b + 1)
                for t in range(TT):
                    claim(f"out{t}", b)
                    for g in range(HG):
                        mm = pe.matmul(half_banks(f"out{t}", b)[:, 0, :], o2T[:, g, t * P:(t + 1) * P],
                                       xwo_sb[:, g, :], start=(g == 0), stop=(g == HG - 1))
                    mm.then_inc(filled(f"out{t}", b), 1)

            def gate_up(b, c, j):
                for w, name in enumerate(("gate", "up")):
                    use = f"{name}{c}{j}"
                    claim(use, b)
                    by_hi = [(wp, x3_hi, k, m) for m in range(2) for k in range(KT) for wp in (wgu_hi, wgu_lo)]
                    by_lo = [(wgu_hi, x3_lo, k, m) for m in range(2) for k in range(KT)]
                    for n, (wp, xp, k, m) in enumerate(by_hi + by_lo):
                        if xp is x3_lo and use == "gate00":
                            wait_drained(pe, "ln3", b)
                        mm = pe.matmul(half_banks(use, b)[:, m, :], wp[:, k, w, c * 4 + 2 * j + m, :],
                                       xp[:, k, :], start=(n == 0), stop=(xp is x3_lo and k == KT - 1),
                                       skip_group_check=True)
                    mm.then_inc(filled(use, b), 1)

            def down(b, c):
                if c == 0:
                    claim("down", b)
                for j in range(4):
                    pe.wait_ge(s_kept, 4 * (FC * b + c) + j + 1)
                    for t in range(TT):
                        mm = pe.matmul(half_banks("down", b)[:, t, :], hidden[:, c, j, t * P:(t + 1) * P],
                                       wd_sb[:, c * 4 + j, :], start=(c == 0 and t == 0 and j == 0),
                                       stop=(c == FC - 1 and j == 3), skip_group_check=True)
                if c == FC - 1:
                    mm.then_inc(filled("down", b), 1)

            def batch(b, more):
                for i in range(HEAD, NQB + LAG_V):
                    if i < NQB:
                        unit_scores(b, i)
                    if i == LN1_AT + 2 and more:
                        transpose_norm("ln1", b, 3 * b + 2)
                    if LAG_T <= i < NQB + LAG_T:
                        unit_transpose(b, i - LAG_T)
                    if i == 8 and more:
                        wait_drained(pe, "ln1", b)
                        rope_group("k0", b, QG)
                    if i == 9 and more:
                        rope_group("k1", b, QG + 1)
                    if i == 11:
                        window_out(b, 0)
                    if i >= LAG_V:
                        unit_values(b, i - LAG_V)
                if more:
                    v_tile("v0", b, 0)
                window_out(b, 1)
                if more:
                    v_tile("v1", b, 1)
                    rope_group("q0", b, 0)
                transpose_norm("ln2", b, 3 * b + (3 if more else 2))
                if more:
                    rope_group("q1", b, 1)
                cross_q(b)
                if more:
                    rope_group("q2", b, 2)
                for i in range(XU + LAG_V):
                    if i in X_FILL and more:
                        rope_group(f"q{X_FILL[i]}", b, X_FILL[i])
                    if i < XU:
                        unit_scores(b, NQB + i)
                    if LAG_T <= i < XU + LAG_T:
                        unit_transpose(b, NQB + i - LAG_T)
                    if i == XU + LAG_V - 1 and more:
                        rope_group("q5", b, 5, halves=(0,))
                    if i >= LAG_V:
                        unit_values(b, NQB + i - LAG_V)
                if more:
                    rope_group("q5", b, 5, halves=(1,))
                cross_out(b)
                if more:
                    rope_group("q6", b, 6)
                    rope_group("q7", b, 7)
                transpose_norm("ln3", b, 3 * b + (4 if more else 3))
                if b == 0:
                    pe.wait_ge(s_wlo, WCHUNKS)
                pe.wait_ge(s_x3hi, b + 1)
                for c in range(FC):
                    for j in range(2):
                        gate_up(b, c, j)
                if more:
                    unit_scores(b + 1, 0)
                    latent_kv(b, b + 2)
                down(b, 0)
                if more:
                    unit_scores(b + 1, 1)
                    unit_scores(b + 1, 2)
                down(b, 1)

            pe.wait_ge(s_ident, 16)
            transpose_norm("ln1", None, 1)
            wait_drained(pe, "ln1", None)
            pe.wait_ge(s_wk, 16 * GROUPS)
            rope_group("k0", None, QG)
            rope_group("k1", None, QG + 1)
            pe.wait_ge(s_wv, 16)
            v_tile("v0", None, 0)
            for g in range(QG):
                pe.wait_ge(s_wq[g // 2], 16)
                rope_group(f"q{g}", None, g)
                if g == QG // 2:
                    v_tile("v1", None, 1)
            pe.wait_ge(s_xkv, 16 * 2)
            latent_kv(None, 1)
            pe.wait_ge(s_cbf, 2)
            pe.wait_ge(s_zero, 2)
            for i in range(HEAD):
                unit_scores(0, i)
            pe.wait_ge(s_wo, 16)
            pe.wait_ge(s_xw, 16 * 2)
            pe.wait_ge(s_wd, 16)
            for b in range(B):
                batch(b, b + 1 < B)

        @block.vector
        def _(dve):
            def row_moments(src, which, n, addend=None, b=None):
                for t in range(TT):
                    if addend:
                        use = f"{addend}{t}"
                        wait_filled(dve, use, b)
                        dve.tensor_tensor(src[:, t, :], half_banks(use, b)[:, 0, :], src[:, t, :], ALU.add)\
                           .then_inc(drained(use, b), 1)
                        wait_drained(dve, use, b)
                    ins = dve.bn_stats(stats[:, which, t, :], src[:, t, :])
                ins.then_inc(s_stats, 1)
                dve.wait_ge(s_stats, n)
                for t in range(TT):
                    ins = dve.bn_aggr(moments[:, which, t, :], stats[:, which, t, :])
                ins.then_inc(s_mom, 1)
                dve.wait_ge(s_mom, n)
                dve.tensor_scalar(vareps[:, which, :], moments[:, which, :, 1], EPS, None,
                                  ALU.add).then_inc(s_var, 1)

            def normalise(src, which, n, prior=None):
                dve.wait_ge(s_rstd, n)
                if prior:
                    wait_filled(dve, *prior)
                for t in range(TT):
                    dve.tensor_scalar(xn[:, t, :], src[:, t, :], moments[:, which, t, 0:1],
                                      rstd[:, which, t:t + 1], ALU.subtract, ALU.mult).then_inc(s_xn, 1)

            def rope_group(name, b, g, n):
                wait_filled(dve, name, b)
                if n > 2:
                    dve.wait_ge(s_addP, pool_sums(n - 2))
                src = half_banks(name, b)
                ring = (n - 1) % 2
                cos, sin = rope[:, ring, 0], rope[:, ring, 1]
                for by, to in enumerate((cos, sin)):
                    ins = dve.tensor_tensor(to, src, trig_sb[:, by:by + 1, :].broadcast_to([P, 2, S]), ALU.mult)
                ins.then_inc(drained(name, b), 1)

            def rope_sums(name, b, g, n):
                wait_drained(dve, name, b)
                ring = (n - 1) % 2
                cos, sin = rope[:, ring, 0], rope[:, ring, 1]
                if g < QG:
                    G, r = g // R, g % R
                    for up in range(2):
                        rows = slice(64 * up, 64 * up + 64)
                        ins = dve.tensor_tensor(qs[64:128, 2 * G + up, :, r], cos[rows, 1, :], sin[rows, 0, :],
                                                ALU.add)
                else:
                    G = g - QG
                    for i in range(4):
                        rows = slice(32 * i, 32 * i + 32)
                        to = 64 + 32 * (i % 2)
                        ins = dve.tensor_tensor(kd[to:to + 32, 2 * G + i // 2, i % 2, WIN:], cos[rows, 1, :],
                                                sin[rows, 0, :], ALU.add)
                ins.then_inc(s_addV, 1)

            def unit_shape(i):
                return dict(g=8 if i < NQB else (4 if i - NQB < XU0 else 2))

            def unit_max(b, i):
                u = UNITS * b + i
                g = unit_shape(i)["g"]
                src = ps[:, BANK_S + i % 2, :].rearrange("p (g k) -> p g k", g=g)
                dve.wait_ge(s_score, u + 1)
                if i >= NQB:
                    dve.tensor_reduce(mx[:, i % ND, 0:g], src, AX.X, ALU.max, negate=True).then_inc(s_max, 1)
                    return
                dve.tensor_reduce(mx[:, i % ND, 0:g], src, AX.X, ALU.max).then_inc(s_max, 1)
                dve.wait_ge(s_max, u + 1)
                if u >= ND:
                    dve.wait_ge(s_tr, u - ND + 1)
                dve.tensor_tensor(prob[:, i % ND, :].rearrange("p (g k) -> p g k", g=g), src,
                                  mx[:, i % ND, 0:g].unsqueeze(2).broadcast_to([P, g, 512 // g]),
                                  ALU.subtract).then_inc(s_sub, 1)

            def unit_sum(b, i):
                u = UNITS * b + i
                g = unit_shape(i)["g"]
                dve.wait_ge(s_exp, u + 1)
                if i < NQB:
                    dve.tensor_reduce(total[:, i % ND, 0:g],
                                      prob[:, i % ND, :].rearrange("p (g k) -> p g k", g=g),
                                      AX.X, ALU.add).then_inc(s_sum, 1)
                    dve.wait_ge(s_sum, NQB * b + i + 1)
                if u >= ND:
                    dve.wait_ge(s_norm, u - ND + 1)
                dve.reciprocal(inv[:, i % ND, 0:g], total[:, i % ND, 0:g]).then_inc(s_inv, 1)

            def chunk_values(b, c, j):
                wait_filled(dve, f"up{c}{j}", b)
                wait_drained(dve, f"gate{c}{j}", b)
                h = hidden[:, c, 2 * j:2 * j + 2, :]
                dve.tensor_tensor(h, h, half_banks(f"up{c}{j}", b), ALU.mult)\
                   .then_inc(drained(f"up{c}{j}", b), 1)

            def sparsify(b, c):
                n = FC * b + c + 1
                dve.wait_ge(s_mag, 2 * n)
                dve.tensor_tensor(beats[:, 0:2, :], mag[:, 0::2, :], mag[:, 1::2, :], ALU.is_ge)
                dve.tensor_tensor(beats[:, 2:4, :], mag[:, 0:2, :], mag[:, 2:4, :], ALU.is_ge)
                dve.tensor_tensor(beats[:, 4, :], mag[:, 0, :], mag[:, 3, :], ALU.is_ge)
                dve.tensor_tensor(beats[:, 5, :], mag[:, 1, :], mag[:, 2, :], ALU.is_ge).then_inc(s_beats, 1)
                dve.wait_ge(s_beats, n)
                b01, b23, b02, b13, b03, b12 = (beats[:, k, :] for k in range(6))
                dve.tensor_tensor(part[:, 0:2, :], beats[:, 2:4, :], beats[:, 4:6, :], ALU.add)
                dve.tensor_tensor(part[:, 2, :], b02, b12, ALU.add)
                dve.tensor_tensor(part[:, 3, :], b13, b03, ALU.add).then_inc(s_part, 1)
                dve.wait_ge(s_part, n)
                dve.tensor_tensor(wins[:, 0, :], part[:, 0, :], b01, ALU.add)
                dve.tensor_tensor(wins[:, 1, :], part[:, 1, :], b01, ALU.subtract)
                dve.tensor_tensor(wins[:, 2, :], b23, part[:, 2, :], ALU.subtract)
                dve.tensor_tensor(wins[:, 3, :], part[:, 3, :], b23, ALU.add).then_inc(s_wins, 1)
                dve.wait_ge(s_wins, n)
                for j, (op, least) in enumerate(((ALU.is_ge, 2.0), (ALU.is_ge, 1.0), (ALU.is_ge, 0.0),
                                                 (ALU.is_le, 1.0))):
                    dve.scalar_tensor_tensor(hidden[:, c, j, :], wins[:, j, :], least, hidden[:, c, j, :],
                                             op, ALU.mult).then_inc(s_kept, 1)

            def add_out(b):
                wait_filled(dve, "down", b)
                dve.tensor_tensor(x_res[:], half_banks("down", b), x_res[:], ALU.add)\
                   .then_inc(drained("down", b), 1)

            def next_group(name, b, g, k):
                n = RG * (b + 1) + k
                rope_group(name, b, g, n)
                rope_sums(name, b, g, n)

            def batch(b, more):
                first = b == 0
                for i in range(HEAD, NQB + LAG_V):
                    if i < NQB:
                        unit_max(b, i)
                    if i <= NQB:
                        unit_sum(b, i - 1)
                    if i == LN1_AT - 1 and more:
                        dve.wait_ge(s_xln, 16 * (b + 2))
                        row_moments(x_ln, 0, 3 * b + 2)
                    if i == LN1_AT and more:
                        normalise(x_ln, 0, 3 * b + 2, ("ln1", None) if first else ("ln3", b - 1))
                    if i == 9 and more:
                        next_group("k0", b, QG, 1)
                    if i == 10 and more:
                        next_group("k1", b, QG + 1, 2)
                dve.wait_ge(s_xres, 16 * (b + 1))
                row_moments(x_res, 1, 3 * b + (3 if more else 2), "wo", b)
                normalise(x_res, 1, 3 * b + (3 if more else 2), ("ln1", b) if more else ("ln3", b - 1))
                if more:
                    for g in range(2):
                        next_group(f"q{g}", b, g, 3 + g)
                for i in range(XU + LAG_V):
                    if i < XU:
                        unit_max(b, NQB + i)
                    if i == 0 and more:
                        next_group("q2", b, 2, 5)
                    if 1 <= i <= XU:
                        unit_sum(b, NQB + i - 1)
                    if i in X_FILL and more:
                        next_group(f"q{X_FILL[i]}", b, X_FILL[i], 3 + X_FILL[i])
                    if 3 <= i < 3 + NQB and more:
                        v_blocks(dve, dve.tensor_copy, b, i - 3)
                if more:
                    next_group("q5", b, 5, 8)
                row_moments(x_res, 2, 3 * b + (4 if more else 3), "out", b)
                normalise(x_res, 2, 3 * b + (4 if more else 3), ("ln2", b))
                if more:
                    rope_group("q6", b, 6, RG * (b + 1) + 9)
                dve.wait_ge(s_x3hi, b + 1)
                dve.tensor_tensor(x3_lo[:], half_banks("ln3", b), x3_hi[:].bitcast(F32), ALU.subtract)\
                   .then_inc(drained("ln3", b), 1)
                if more:
                    rope_sums("q6", b, 6, RG * (b + 1) + 9)
                    next_group("q7", b, 7, 10)
                for j in range(2):
                    chunk_values(b, 0, j)
                sparsify(b, 0)
                for j in range(2):
                    chunk_values(b, 1, j)
                if more:
                    unit_max(b + 1, 0)
                sparsify(b, 1)
                if more:
                    for i in range(1, HEAD):
                        unit_max(b + 1, i)
                        unit_sum(b + 1, i - 1)
                add_out(b)

            dve.wait_ge(s_xln, 16)
            row_moments(x_ln, 0, 1)
            normalise(x_ln, 0, 1)
            dve.memset(v2z[:], 0.0).then_inc(s_zero, 1)
            dve.wait_ge(s_ident, 16)
            dve.tensor_copy(ident_bf[:], ident_sb[:]).then_inc(s_cbf, 1)
            dve.wait_ge(s_zero, 2)
            dve.wait_ge(s_trig, 16)
            for g in range(GROUPS):
                rope_group(f"k{g}", None, QG + g, g + 1)
                rope_sums(f"k{g}", None, QG + g, g + 1)
            for g in range(QG):
                rope_group(f"q{g}", None, g, GROUPS + g + 1)
                rope_sums(f"q{g}", None, g, GROUPS + g + 1)
                if g == QG // 2:
                    dve.wait_ge(s_masks, 32)
                    dve.tensor_copy(mask_sb[:], mask_f[:]).then_inc(s_cbf, 1)
            unit_max(0, 0)
            for i in range(1, HEAD):
                unit_max(0, i)
                unit_sum(0, i - 1)
            for b in range(B):
                batch(b, b + 1 < B)

        @block.gpsimd
        def _(pool):
            def inverse_root(which, n):
                pool.wait_ge(s_var, n)
                pool.tensor_tensor(rstd[:, which, :], vareps[:, which, :], power[:], ALU.pow).then_inc(s_rstd, 1)

            def rope_sums(name, b, g, n):
                wait_drained(pool, name, b)
                ring = (n - 1) % 2
                cos, sin = rope[:, ring, 0], rope[:, ring, 1]
                done = pool_sums(n - 1)
                if g < QG:
                    G, r = g // R, g % R
                    for up in range(2):
                        if done + up:
                            pool.wait_ge(s_addP, done + up)
                        rows = slice(64 * up, 64 * up + 64)
                        pool.tensor_tensor(qs[0:64, 2 * G + up, :, r], cos[rows, 0, :], sin[rows, 1, :],
                                           ALU.subtract).then_inc(s_addP, 1)
                else:
                    G = g - QG
                    for i in range(4):
                        if done + i:
                            pool.wait_ge(s_addP, done + i)
                        rows = slice(32 * i, 32 * i + 32)
                        to = 32 * (i % 2)
                        pool.tensor_tensor(kd[to:to + 32, 2 * G + i // 2, i % 2, WIN:], cos[rows, 0, :],
                                           sin[rows, 1, :], ALU.subtract).then_inc(s_addP, 1)

            def unit_norm(b, i):
                u = UNITS * b + i
                g = 8 if i < NQB else (4 if i - NQB < XU0 else 2)
                pool.wait_ge(s_inv, u + 1)
                p = prob[:, i % ND, :].rearrange("p (g k) -> p g k", g=g)
                pool.tensor_tensor(p, p, inv[:, i % ND, 0:g].unsqueeze(2).broadcast_to([P, g, 512 // g]),
                                   ALU.mult).then_inc(s_norm, 1)

            def cross_keys(b, h):
                if h == 0:
                    wait_drained(pool, "xk", before(b))
                ins = pool.tensor_tensor(k2d[:, 1, h, :], k2T[:, 1, :],
                                         rowmask_sb[:, h:h + 1].broadcast_to([P, S]), ALU.mult)
                if h == HPT - 1:
                    ins.then_inc(s_k2v, 1)

            def split_weights(c):
                pool.wait_ge(s_whi, c + 1)
                pool.tensor_tensor(lo_c[c], raw[:, c % RAW, :], hi_c[c].bitcast(F32), ALU.subtract)\
                    .then_inc(s_wlo, 1)

            def next_group(name, b, g, k):
                rope_sums(name, b, g, RG * (b + 1) + k)

            def after_sums(b, k):
                pool.wait_ge(s_addP, pool_sums(RG) * (b + 1) + pool_sums(k))

            def batch(b, more):
                after_sums(b, 0)
                for i in range(NQB):
                    if i == LN1_AT - 1 and more:
                        inverse_root(0, 3 * b + 2)
                    unit_norm(b, i)
                    cross_keys(b, i)
                if more:
                    pool.wait_ge(s_norm, UNITS * b + NQB)
                    next_group("k0", b, QG, 1)
                    next_group("k1", b, QG + 1, 2)
                    after_sums(b, 2)
                inverse_root(1, 3 * b + (3 if more else 2))
                if more:
                    pool.wait_ge(s_rstd, 3 * b + 3)
                    for g in range(3):
                        next_group(f"q{g}", b, g, 3 + g)
                    after_sums(b, 5)
                for i in range(XU + LAG_V):
                    if b == 0 and 1 <= i <= WCHUNKS:
                        split_weights(i - 1)
                    if 1 <= i <= XU:
                        unit_norm(b, NQB + i - 1)
                    if i in X_FILL and more:
                        pool.wait_ge(s_norm, UNITS * b + NQB + min(i, XU))
                        g = X_FILL[i]
                        next_group(f"q{g}", b, g, 3 + g)
                        after_sums(b, 3 + g)
                if more:
                    pool.wait_ge(s_norm, UNITS * (b + 1))
                    next_group("q5", b, 5, 8)
                    after_sums(b, 8)
                inverse_root(2, 3 * b + (4 if more else 3))
                if more:
                    pool.wait_ge(s_rstd, 3 * b + 4)
                    for g in range(6, QG):
                        next_group(f"q{g}", b, g, 3 + g)

            pool.memset(power[:], -0.5).then_inc(s_power, 1)
            pool.wait_ge(s_power, 1)
            inverse_root(0, 1)
            pool.memset(kd[:], 0.0)
            pool.memset(vb[:], 0.0).then_inc(s_zero, 1)
            pool.wait_ge(s_zero, 2)
            for g in range(GROUPS):
                rope_sums(f"k{g}", None, QG + g, g + 1)
            for g in range(QG):
                rope_sums(f"q{g}", None, g, GROUPS + g + 1)
            pool.wait_ge(s_masks, 32)
            for b in range(B):
                batch(b, b + 1 < B)

        @block.scalar
        def _(act):
            def copy_norm(name, b, which):
                wait_filled(act, name, b)
                act.activation(xnT[:, which], half_banks(name, b), ACT.Copy)\
                   .then_inc(drained(name, b), 1)

            def v_copy(name, b, t):
                wait_filled(act, name, b)
                act.activation(v_sb[:, t, :], bank(name, b), ACT.Copy).then_inc(drained(name, b), 1)

            def unit_exp(b, i):
                u = UNITS * b + i
                if i < NQB:
                    act.wait_ge(s_sub, NQB * b + i + 1)
                    act.activation(prob[:, i % ND, :], prob[:, i % ND, :], ACT.Exp, scale=HD ** -0.5)\
                       .then_inc(s_exp, 1)
                    return
                act.wait_ge(s_max, u + 1)
                act.wait_ge(s_tr, u - ND + 1)
                g = 4 if i - NQB < XU0 else 2
                k = 512 // g
                for h in range(g):
                    ins = act.activation(prob[:, i % ND, h * k:(h + 1) * k],
                                         ps[:, BANK_S + i % 2, h * k:(h + 1) * k], ACT.Exp,
                                         bias=mx[:, i % ND, h:h + 1], accum_out=total[:, i % ND, h:h + 1])
                ins.then_inc(s_exp, 1)

            def unit_pT(b, i):
                u = UNITS * b + i
                act.wait_ge(s_tr, u + 1)
                if u >= 2:
                    act.wait_ge(s_av, u - 1)
                act.activation(pT[:, i % 2, :], ps[:, BANK_PT + i % 2, :], ACT.Copy).then_inc(s_pT, 1)

            def unit_out(b, i):
                act.wait_ge(s_av, UNITS * b + i + 1)
                act.activation(qs_rows[:, :, i * P:(i + 1) * P],
                               ps[:, BANK_O, :].rearrange("p (c n) -> p c n", c=PAIRS), ACT.Copy).then_inc(s_oT, 1)

            def latent_kv(b):
                wait_filled(act, "xk", b)
                act.activation(k2T[:], half_banks("xk", b), ACT.Copy).then_inc(drained("xk", b), 1)
                wait_filled(act, "xv", b)
                src = half_banks("xv", b).rearrange("p t (h e d) -> p t h e d", h=XH // 2, e=2)
                for e in range(2):
                    for t in range(TT):
                        ins = act.activation(v2z[:, t, e::2, e * XD:(e + 1) * XD], src[:, t, :, e, :], ACT.Copy)
                ins.then_inc(drained("xv", b), 1)

            def cross_keys(b, h):
                if h == 0:
                    wait_drained(act, "xk", before(b))
                ins = act.activation(k2d[:, 0, h, :], k2T[:, 0, :], ACT.Copy, scale=rowmask_sb[:, h:h + 1])
                if h == HPT - 1:
                    ins.then_inc(s_k2a, 1)

            def round_weights(c):
                act.wait_ge(s_wraw[c % RAW], 16 * (c // RAW + 1))
                act.activation(hi_c[c], raw[:, c % RAW, :], ACT.Copy).then_inc(s_whi, 1)

            def gate(b, c, j):
                use = f"gate{c}{j}"
                wait_filled(act, use, b)
                act.activation(hidden[:, c, 2 * j:2 * j + 2, :], half_banks(use, b), ACT.Silu)\
                   .then_inc(drained(use, b), 1)

            def magnitudes(b, c, j):
                wait_drained(act, f"up{c}{j}", b)
                if c:
                    act.wait_ge(s_beats, FC * b + c)
                act.activation(mag[:, 2 * j:2 * j + 2, :], hidden[:, c, 2 * j:2 * j + 2, :], ACT.Abs)\
                   .then_inc(s_mag, 1)

            def batch(b, more):
                for i in range(HEAD, NQB + LAG_V):
                    if LAG_T <= i < NQB + LAG_T:
                        unit_pT(b, i - LAG_T)
                    if i >= LAG_V:
                        unit_out(b, i - LAG_V)
                    if i < NQB:
                        unit_exp(b, i)
                    if i == LN1_AT + 2 and more:
                        copy_norm("ln1", b, 0)
                    if 3 <= i < 3 + HPT:
                        cross_keys(b, i - 3)
                    if b == 0 and 0 <= i - HEAD < RAW:
                        round_weights(i - HEAD)
                if more:
                    v_copy("v0", b, 0)
                    v_copy("v1", b, 1)
                copy_norm("ln2", b, 1)
                wait_filled(act, "xq", b)
                act.activation(q2T[:], half_banks("xq", b), ACT.Copy, scale=XD ** -0.5)\
                   .then_inc(drained("xq", b), 1)
                for i in range(XU + LAG_T):
                    if i >= LAG_T:
                        unit_pT(b, NQB + i - LAG_T)
                    if i < XU:
                        unit_exp(b, NQB + i)
                    if b == 0 and RAW <= i < WCHUNKS:
                        round_weights(i)
                act.wait_ge(s_av, UNITS * (b + 1))
                act.activation(o2T[:], ps[:, BANK_O, :].rearrange("p (g s) -> p g s", g=HG), ACT.Copy)\
                   .then_inc(s_o2T, 1)
                wait_filled(act, "ln3", b)
                act.activation(x3_hi[:], half_banks("ln3", b), ACT.Copy).then_inc(s_x3hi, 1)
                for c in range(FC):
                    for j in range(2):
                        gate(b, c, j)
                    for j in range(2):
                        magnitudes(b, c, j)
                if more:
                    unit_exp(b + 1, 0)
                    latent_kv(b)
                    for i in range(1, HEAD):
                        unit_exp(b + 1, i)
                    wait_filled(act, "down", b)

            copy_norm("ln1", None, 0)
            v_copy("v0", None, 0)
            v_copy("v1", None, 1)
            act.wait_ge(s_zero, 2)
            for q in range(NQB):
                v_blocks(act, act.copy, None, q)
            latent_kv(None)
            act.wait_ge(s_masks, 32)
            for i in range(HEAD):
                unit_exp(0, i)
            for b in range(B):
                batch(b, b + 1 < B)


def constants():
    inv_freq = (1.0 / np.float32(10000.0) ** (np.arange(0, HD, 2, dtype=np.float32) / np.float32(HD)))
    angle = np.arange(S, dtype=np.float32)[:, None] * inv_freq.astype(np.float32)[None, :]
    cos, sin = np.cos(angle).T, np.sin(angle).T
    trig = np.tile(np.stack([cos, sin], axis=1), (4, 1, 1)).astype(np.float32)
    q, k = np.arange(QB)[:, None], np.arange(WK)[None, :]
    hidden = (k > WIN + q) | (k < q)
    first = hidden | (k < WIN)
    later = np.arange(P)[None, :] > np.arange(P)[:, None]
    masks = np.concatenate([np.repeat(first, R, 0), np.repeat(hidden, R, 0), later], axis=1)
    masks = np.where(masks, MASKED, 0.0).astype(np.float32)
    rowmask = (np.arange(P)[:, None] // XD == np.arange(HPT)[None, :]).astype(np.float32)
    return trig, masks, np.eye(P, dtype=np.float32), rowmask


def kernel(x, ctx_512, L0_attn_wq, L0_attn_wk, L0_attn_wv, L0_attn_wo, L0_xattn_Wq, L0_xattn_Wkv_expand,
           L0_xattn_Wout, L0_ffn_w_gate, L0_ffn_w_up, L0_ffn_w_down):
    import concourse.bacc as bacc
    from concourse.bass_utils import run_bass_kernel_spmd

    a = np.asarray
    q = a(L0_attn_wq).reshape(GROUPS, 4, R, 2, HALF, D).transpose(5, 0, 2, 3, 1, 4).reshape(D, QG, 2, P)
    k = a(L0_attn_wk).reshape(GROUPS, 4, 2, HALF, D).transpose(4, 0, 2, 1, 3).reshape(D, GROUPS, 2, P)
    by_k = lambda w: w.reshape(KT, P, *w.shape[1:]).swapaxes(0, 1)
    ffn = lambda w: by_k(a(w).reshape(D, FC, P, 4).transpose(0, 1, 3, 2).reshape(D, FC * 4, P))
    trig, masks, ident, rowmask = constants()
    arrays = {
        "x": a(x),
        "ctxT": a(ctx_512)[:, :S].transpose(0, 2, 1),
        "wqk": by_k(np.concatenate([q, k], axis=1)),
        "wv": by_k(a(L0_attn_wv).T),
        "wo": a(L0_attn_wo).T.reshape(PAIRS, 2, R, HD, D).transpose(1, 3, 0, 2, 4).reshape(P, PAIRS, R, D),
        "xwq": by_k(a(L0_xattn_Wq).T),
        "xwk": a(L0_xattn_Wkv_expand)[:D].T,
        "xwv": a(L0_xattn_Wkv_expand)[D:].T,
        "xwo": by_k(a(L0_xattn_Wout).T),
        "wgu": np.stack([ffn(L0_ffn_w_gate), ffn(L0_ffn_w_up)], axis=2),
        "wd": a(L0_ffn_w_down).reshape(FC, P, 4, D).transpose(1, 0, 2, 3).reshape(P, FC * 4, D),
        "trig": trig, "masks": masks, "ident": ident, "rowmask": rowmask,
    }
    nc = bacc.Bacc("TRN2", target_bir_lowering=False, num_devices=1)
    args, feeds = {}, {}
    for name, v in arrays.items():
        feeds[f"in_{name}"] = np.ascontiguousarray(v)
        args[name] = nc.dram_tensor(f"in_{name}", v.shape, F32, kind="ExternalInput").ap()
    args["out"] = nc.dram_tensor("out_0", (B, S, D), F32, kind="ExternalOutput").ap()
    build(nc, **args)
    r = run_bass_kernel_spmd(nc, [feeds], core_ids=[0])
    return r.results[0]["out_0"]
```

```python
from contextlib import ExitStack

import numpy as np

import concourse.bass as bass
from concourse import mybir

ALU = mybir.AluOpType
ACT = mybir.ActivationFunctionType
AX = mybir.AxisListType
F32 = mybir.dt.float32
F32R = mybir.dt.float32r
BF16 = mybir.dt.bfloat16

P = 128
B, S, D = 4, 256, 256
KT = D // P
TT = S // P
H, KV, HD = 32, 8, 64
R = H // KV
HALF = HD // 2
WIN = 32
QB = 32
NQB = S // QB
WK = QB + WIN
PAIRS = KV // 2
GROUPS = KV // 4
QG = GROUPS * R
RG = QG + GROUPS
XH, XD, L = 16, 16, 64
HG = XH * XD // P
HPT = P // XD
XU0, XU1 = 4, 8
XU = XU0 + XU1
WCHUNKS = 8
RAW = 4
UNITS = NQB + XU
FF = 1024
FC = FF // (4 * P)
EPS = 1e-5
MASKED = -1.0e37
LAG_T, LAG_V = 3, 4
ND = 4
HEAD = 3
X_FILL = {2: 2, 4: 3, 13: 4}
OUT0_AT = 9
SPLITS = 5

BANK_S, BANK_PT, BANK_O, BANK_M = 0, 2, 4, 5
NM = 3
NF = 3

NEXT_USES = ["ln1", "k0", "k1", "v0", "q0", "q1", "q2", "q3", "q4", "v1", "q5", "q6", "q7", "xk", "xv"]
USES = ["wo0", "ln1", "v0", "wo1", "v1", "k0", "ln20", "k1", "xq0", "q0", "ln21", "q1", "xq1", "q2", "q3",
        "out0", "q4", "q5", "out1", "q6", "q7", "ln3", "xk", "xv", "down"]
FFN_USES = [f"{w}{c}{j}" for c in range(FC) for j in range(2) for w in ("gate", "up")]
ORDER = [(u, None) for u in NEXT_USES] + [(u, b) for b in range(B) for u in USES
                                          if b + 1 < B or u not in NEXT_USES]
FFN_ORDER = [(u, b) for b in range(B) for u in FFN_USES]


def ring_use(name, b):
    if name in FFN_USES:
        n = FFN_ORDER.index((name, b))
        return NM + n % NF, n // NF
    n = ORDER.index((name, b))
    return n % NM, n // NM


def pool_sums(n):
    batches, m = divmod(n, RG)
    return batches * (4 * GROUPS + 2 * QG) + (4 * m if m <= GROUPS else 4 * GROUPS + 2 * (m - GROUPS))


def build(nc, x, ctxT, wqk, wv, wo, xwq, xwk, xwv, xwo, wgu, wd, trig, masks, ident, rowmask, out):
    es = ExitStack()
    with es:
        def sb(name, shape, dt=F32):
            return es.enter_context(nc.sbuf_tensor(name, shape, dt))

        def sem(name):
            return es.enter_context(nc.semaphore(name))

        wqk_sb = sb("wqk_sb", [P, KT, RG, 2, P])
        wv_sb = sb("wv_sb", [P, KT, KV * HD])
        wo_sb = sb("wo_sb", [P, PAIRS, R, D])
        xwq_sb = sb("xwq_sb", [P, KT, D])
        xwk_sb = sb("xwk_sb", [L, D])
        xwv_sb = sb("xwv_sb", [L, D])
        xwo_sb = sb("xwo_sb", [P, HG, D])
        wgu_hi = sb("wgu_hi", [P, KT, 2, FC * 4, P], F32R)
        wgu_lo = sb("wgu_lo", [P, KT, 2, FC * 4, P], F32R)
        wd_sb = sb("wd_sb", [P, FC * 4, D])
        trig_sb = sb("trig_sb", [P, 2, S])
        mask_sb = sb("mask_sb", [P, 2 * WK + P], BF16)
        mask_f = sb("mask_f", [P, 2 * WK + P])
        ident_sb = sb("ident_sb", [P, P])
        ident_bf = sb("ident_bf", [P, P], BF16)
        rowmask_sb = sb("rowmask_sb", [P, HPT])
        wcols = KT * 2 * FC * 4 * P // WCHUNKS
        raw = sb("raw", [P, RAW, wcols])
        x_ln = sb("x_ln", [P, TT, D])
        x_res = sb("x_res", [P, TT, D])
        stats = sb("stats", [P, 3, TT, 6])
        moments = sb("moments", [P, 3, TT, 2])
        vareps = sb("vareps", [P, 3, TT])
        power = sb("power", [P, 1])
        rstd = sb("rstd", [P, 3, TT])
        xn = sb("xn", [P, TT, D])
        xnT = sb("xnT", [P, 2, KT, S])
        x3_hi = sb("x3_hi", [P, KT, S], F32R)
        x3_lo = sb("x3_lo", [P, KT, S], F32R)
        rope = sb("rope", [P, 2, 2, 2, S])
        qs = sb("qs", [P, PAIRS, S, R])
        qs_rows = qs[:].rearrange("p c s r -> p c (s r)")
        kd = sb("kd", [P, PAIRS, 2, WIN + S])
        v_sb = sb("v_sb", [P, TT, KV * HD])
        vb = sb("vb", [P, NQB, PAIRS, 2 * HD])
        prob = sb("prob", [P, ND, 512])
        mx = sb("mx", [P, ND, 8])
        total = sb("total", [P, ND, 8])
        inv = sb("inv", [P, ND, 8])
        pT = sb("pT", [P, 2, 512])
        ctx_sb = sb("ctx_sb", [L, S])
        k2T = sb("k2T", [P, HG, S])
        k2d = sb("k2d", [P, HG, HPT, S])
        v2z = sb("v2z", [P, TT, XH, 2 * XD])
        q2T = sb("q2T", [P, HG, S])
        o2T = q2T
        work = k2d[:].rearrange("p g h s -> p (g h) s")
        hidden = work[:, 0:4 * FC, :].rearrange("p (c j) s -> p c j s", c=FC)
        mag = work[:, 4 * FC:4 * FC + 4, :]
        beats = work[:, 4 * FC + 4:4 * FC + 7, :].bitcast(BF16).rearrange("p a (b s) -> p (a b) s", b=2)
        part = sb("part", [P, 4, S], BF16)
        wins = sb("wins", [P, 4, S], BF16)

        ps = es.enter_context(nc.psum_tensor("ps", [P, 8, 512], F32))

        s_ident = sem("s_ident")
        s_trig = sem("s_trig")
        s_masks = sem("s_masks")
        s_wk = sem("s_wk")
        s_wq = [sem(f"s_wq{k}") for k in range(QG // 2)]
        s_wv = sem("s_wv")
        s_wrest = [sem(f"s_w{n}") for n in ("wo", "xattn", "d")]
        s_wo, s_xw, s_wd = s_wrest
        s_xkv = sem("s_xkv")
        s_xln = sem("s_xln")
        s_xres = sem("s_xres")
        s_ctx = sem("s_ctx")
        s_zero = sem("s_zero")
        s_cbf = sem("s_cbf")
        s_filled = [sem(f"s_filled{k}") for k in range(NM + NF)]
        s_drained = [sem(f"s_drained{k}") for k in range(NM + NF)]
        s_stats = sem("s_stats")
        s_mom = sem("s_mom")
        s_power = sem("s_power")
        s_var = sem("s_var")
        s_rstd = sem("s_rstd")
        s_xn = sem("s_xn")
        s_addP = sem("s_addP")
        s_addV = sem("s_addV")
        s_vb = sem("s_vb")
        s_x3hi = sem("s_x3hi")
        s_wraw = [sem(f"s_wraw{k}") for k in range(RAW)]
        s_whi = sem("s_whi")
        s_wlo = sem("s_wlo")
        s_score = sem("s_score")
        s_max = sem("s_max")
        s_sub = sem("s_sub")
        s_exp = sem("s_exp")
        s_sum = sem("s_sum")
        s_inv = sem("s_inv")
        s_norm = sem("s_norm")
        s_tr = sem("s_tr")
        s_pT = sem("s_pT")
        s_av = sem("s_av")
        s_oT = sem("s_oT")
        s_k2a = sem("s_k2a")
        s_k2v = sem("s_k2v")
        s_o2T = sem("s_o2T")
        s_mag = sem("s_mag")
        s_beats = sem("s_beats")
        s_part = sem("s_part")
        s_wins = sem("s_wins")
        s_kept = sem("s_kept")
        s_out = sem("s_out")

        def bank(name, b):
            k, _ = ring_use(name, b)
            return ps[:, BANK_M + k if k < NM else BANK_PT + k - NM, :]

        def half_banks(name, b):
            return bank(name, b).rearrange("p (t n) -> p t n", t=2)

        def quarter_banks(name, b):
            return bank(name, b).rearrange("p (t n) -> p t n", t=4)

        def wait_filled(eng, name, b):
            k, n = ring_use(name, b)
            eng.wait_ge(s_filled[k], n + 1)

        def wait_drained(eng, name, b):
            k, n = ring_use(name, b)
            eng.wait_ge(s_drained[k], n + 1)

        def before(b):
            return b - 1 if b else None

        def filled(name, b):
            return s_filled[ring_use(name, b)[0]]

        def drained(name, b):
            return s_drained[ring_use(name, b)[0]]

        flat = lambda w: w.rearrange("p k w c n -> p (k w c n)")
        wgu_c = [flat(wgu)[:, c * wcols:(c + 1) * wcols] for c in range(WCHUNKS)]
        hi_c = [flat(wgu_hi[:])[:, c * wcols:(c + 1) * wcols] for c in range(WCHUNKS)]
        lo_c = [flat(wgu_lo[:])[:, c * wcols:(c + 1) * wcols] for c in range(WCHUNKS)]

        def v_blocks(eng, copy, b, q):
            if q % (P // QB) == 0:
                wait_drained(eng, f"v{q // (P // QB)}", b)
            rows = slice(q % (P // QB) * QB, q % (P // QB) * QB + QB)
            src = v_sb[rows, q // (P // QB), :].rearrange("p (c e d) -> p c e d", c=PAIRS, e=2)
            for e in range(2):
                for own in range(2 if q + 1 < NQB else 1):
                    u = q + own
                    to = 64 * e + WIN * (1 - own)
                    ins = copy(vb[to:to + QB, u, :, e * HD:(e + 1) * HD], src[:, :, e, :])
            if q == NQB - 1:
                ins.then_inc(s_vb, 1)

        block = es.enter_context(nc.Block())

        @block.sync
        def _(sp):
            def load_x(b):
                return x[b].rearrange("(t p) d -> p t d", p=P)

            sp.dma_start(x_ln[:], load_x(0)).then_inc(s_xln, 16)
            sp.dma_start(ident_sb[:], ident).then_inc(s_ident, 16)
            for g in (QG, QG + 1):
                sp.dma_start(wqk_sb[:, :, g], wqk[:, :, g]).then_inc(s_wk, 16)
            sp.dma_start(trig_sb[:], trig).then_inc(s_trig, 16)
            sp.dma_start(wv_sb[:], wv).then_inc(s_wv, 16)
            for g in range(0, QG, 2):
                sp.dma_start(wqk_sb[:, :, g:g + 2], wqk[:, :, g:g + 2]).then_inc(s_wq[g // 2], 16)
            sp.dma_start(mask_f[:], masks).then_inc(s_masks, 16)
            sp.dma_start(rowmask_sb[:], rowmask).then_inc(s_masks, 16)
            sp.dma_start(xwk_sb[:], xwk).then_inc(s_xkv, 16)
            sp.dma_start(xwv_sb[:], xwv).then_inc(s_xkv, 16)
            sp.dma_start(ctx_sb[:], ctxT[0]).then_inc(s_ctx, 16)
            sp.dma_start(x_res[:], load_x(0)).then_inc(s_xres, 16)
            sp.dma_start(wo_sb[:], wo).then_inc(s_wo, 16)
            sp.dma_start(xwq_sb[:], xwq).then_inc(s_xw, 16)
            sp.dma_start(xwo_sb[:], xwo).then_inc(s_xw, 16)
            for c in range(RAW):
                sp.dma_start(raw[:, c, :], wgu_c[c]).then_inc(s_wraw[c], 16)
            sp.dma_start(wd_sb[:], wd).then_inc(s_wd, 16)

            sp.wait_ge(s_xn, TT)
            sp.dma_start(x_ln[:], load_x(1)).then_inc(s_xln, 16)
            wait_filled(sp, "xv", None)
            sp.dma_start(ctx_sb[:], ctxT[1]).then_inc(s_ctx, 16)
            for b in range(B):
                if b + 2 < B:
                    sp.wait_ge(s_xn, TT * (3 * b + 2))
                    sp.dma_start(x_ln[:], load_x(b + 2)).then_inc(s_xln, 16)
                if b == 0:
                    for c in range(RAW, WCHUNKS):
                        sp.wait_ge(s_wlo, c - RAW + 1)
                        sp.dma_start(raw[:, c % RAW, :], wgu_c[c]).then_inc(s_wraw[c % RAW], 16)
                if b + 2 < B:
                    wait_filled(sp, "xv", b)
                    sp.dma_start(ctx_sb[:], ctxT[b + 2]).then_inc(s_ctx, 16)
                wait_drained(sp, "down", b)
                sp.dma_start(out[b].rearrange("(t p) d -> p t d", p=P), x_res[:]).then_inc(s_out, 16)
                if b + 1 < B:
                    sp.wait_ge(s_out, 16 * (b + 1))
                    sp.dma_start(x_res[:], load_x(b + 1)).then_inc(s_xres, 16)
            sp.wait_ge(s_out, 16 * B)

        @block.tensor
        def _(pe):
            def claim(name, b):
                k, n = ring_use(name, b)
                if n:
                    pe.wait_ge(s_drained[k], n)

            def transpose_norm(name, b, n):
                claim(name, b)
                o = half_banks(name, b)
                for t in range(TT):
                    mm = transpose_tile(o[:, :, t * P:(t + 1) * P], t, n)
                mm.then_inc(filled(name, b), 1)

            def transpose_tile(o, t, n):
                pe.wait_ge(s_xn, TT * (n - 1) + t + 1)
                for k in range(KT):
                    mm = pe.transpose(o[:, k, :], xn[:, t, k * P:(k + 1) * P], ident_sb[:])
                return mm

            def rope_group(name, b, g, halves=(0, 1)):
                if 0 in halves:
                    claim(name, b)
                o = half_banks(name, b)
                for half in halves:
                    for k in range(KT):
                        mm = pe.matmul(o[:, half, :], wqk_sb[:, k, g, half, :], xnT[:, 0, k, :],
                                       start=(k == 0), stop=(k == KT - 1))
                if 1 in halves:
                    mm.then_inc(filled(name, b), 1)

            def v_tile(name, b, t):
                claim(name, b)
                for k in range(KT):
                    mm = pe.matmul(bank(name, b), xnT[:, 0, k, t * P:(t + 1) * P], wv_sb[:, k, :],
                                   start=(k == 0), stop=(k == KT - 1))
                mm.then_inc(filled(name, b), 1)

            def unit_scores(b, i):
                u = UNITS * b + i
                if u >= 2:
                    if i < 2:
                        pe.wait_ge(s_exp, u - 1)
                    elif i < NQB + 2:
                        pe.wait_ge(s_sub, NQB * b + i - 1)
                    else:
                        pe.wait_ge(s_exp, u - 1)
                o = ps[:, BANK_S + i % 2, :]
                if i < NQB:
                    if i == 0:
                        pe.wait_ge(s_addP, pool_sums(RG) * (b + 1))
                        pe.wait_ge(s_addV, RG * (b + 1))
                    at = 0 if i == 0 else WK
                    pe.matmul(o, ident_bf[:], mask_sb[:, at:at + WK].unsqueeze(1).broadcast_to([P, KV, WK]),
                              start=True, stop=False, skip_group_check=True)
                    for p in range(PAIRS):
                        mm = pe.matmul(o[:, p * P:(p + 1) * P], qs_rows[:, p, i * P:(i + 1) * P],
                                       kd[:, p, :, i * QB:i * QB + WK], start=False, stop=(p == PAIRS - 1),
                                       skip_group_check=True)
                else:
                    j = i - NQB
                    if j == 0:
                        wait_drained(pe, "xq0", b)
                        pe.wait_ge(s_k2a, b + 1)
                    if j == XU0:
                        wait_drained(pe, "xq1", b)
                    if j == XU0 // HG:
                        pe.wait_ge(s_k2v, b + 1)
                    tile = 0 if j < XU0 else 1
                    n = 4 if tile == 0 else 2
                    h0 = j * 4 if tile == 0 else (j - XU0) * 2
                    pe.matmul(o.rearrange("p (g k) -> p g k", g=n)[:, :, tile * P:(tile + 1) * P], ident_bf[:],
                              mask_sb[:, 2 * WK:].unsqueeze(1).broadcast_to([P, n, P]), start=True, stop=False,
                              skip_group_check=True)
                    mm = pe.matmul(o, q2T[:, h0 // HPT, tile * P:(tile + 1) * P],
                                   k2d[:, h0 // HPT, h0 % HPT:h0 % HPT + n, 0:(tile + 1) * P],
                                   start=False, stop=True, skip_group_check=True)
                mm.then_inc(s_score, 1)

            def ffn_banks_free(b):
                for use in FFN_USES[-NF:]:
                    wait_drained(pe, use, b - 1)

            def unit_transpose(b, i):
                u = UNITS * b + i
                pe.wait_ge(s_norm, u + 1)
                if b and i < 2:
                    ffn_banks_free(b)
                if u >= 2:
                    pe.wait_ge(s_pT, u - 1)
                for c in range(4):
                    mm = pe.transpose(ps[:, BANK_PT + i % 2, c * P:(c + 1) * P],
                                      prob[:, i % ND, c * P:(c + 1) * P], ident_sb[:])
                mm.then_inc(s_tr, 1)

            def unit_values(b, i):
                u = UNITS * b + i
                pe.wait_ge(s_pT, u + 1)
                pT_i = pT[:, i % 2, :].rearrange("p (c n) -> p c n", c=4)
                if i < NQB:
                    if i == 0:
                        pe.wait_ge(s_vb, b + 1)
                        if b:
                            pe.wait_ge(s_o2T, TT * b)
                    else:
                        pe.wait_ge(s_oT, NQB * b + i)
                    for p in range(PAIRS):
                        mm = pe.matmul(ps[:, BANK_O, p * P:(p + 1) * P], vb[:, i, p, :], pT_i[:, p, :],
                                       start=True, stop=True)
                else:
                    j = i - NQB
                    if j == 0:
                        wait_drained(pe, "xv", before(b))
                        pe.wait_ge(s_oT, NQB * (b + 1))
                    if j == XU0:
                        pe.wait_ge(s_o2T, TT * b + 1)
                    tile = 0 if j < XU0 else 1
                    h0 = j * 4 if tile == 0 else (j - XU0) * 2
                    for pair in range(2 - tile):
                        quad = (h0 + 2 * pair) % HPT // 2
                        o = ps[32 * quad:32 * quad + 32, BANK_O, :].rearrange("p (g s) -> p g s", g=HG)
                        n = 0
                        for h in range(2):
                            for kt in range(tile + 1):
                                c = (2 * pair + h) if tile == 0 else 2 * h + kt
                                mm = pe.matmul(o[:, h0 // HPT, tile * P:(tile + 1) * P],
                                               v2z[:, kt, h0 + 2 * pair + h, :], pT_i[:, c, :],
                                               start=(n == 0), stop=(n == 2 * (tile + 1) - 1))
                                n += 1
                mm.then_inc(s_av, 1)

            def window_out(b, t, pair):
                use = f"wo{t}"
                if pair == 0:
                    claim(use, b)
                    pe.wait_ge(s_oT, NQB * b + NQB // TT * (t + 1))
                for r in range(R):
                    mm = pe.matmul(half_banks(use, b)[:, 0, :], qs[:, pair, t * P:(t + 1) * P, r],
                                   wo_sb[:, pair, r, :], start=(pair == 0 and r == 0),
                                   stop=(pair == PAIRS - 1 and r == R - 1))
                if pair == PAIRS - 1:
                    mm.then_inc(filled(use, b), 1)

            def latent_kv(b, n):
                pe.wait_ge(s_ctx, 16 * n)
                claim("xk", b)
                for g in range(HG):
                    mm = pe.matmul(half_banks("xk", b)[:, g, :], xwk_sb[:, g * P:(g + 1) * P], ctx_sb[:],
                                   start=True, stop=True)
                mm.then_inc(filled("xk", b), 1)
                claim("xv", b)
                for t in range(TT):
                    mm = pe.matmul(half_banks("xv", b)[:, t, :], ctx_sb[:, t * P:(t + 1) * P], xwv_sb[:],
                                   start=True, stop=True)
                mm.then_inc(filled("xv", b), 1)

            def cross_norm(b, t, n):
                claim(f"ln2{t}", b)
                transpose_tile(quarter_banks(f"ln2{t}", b)[:, 0:KT, :], t, n).then_inc(filled(f"ln2{t}", b), 1)

            def cross_q(b, t):
                claim(f"xq{t}", b)
                wait_drained(pe, f"ln2{t}", b)
                for g in range(HG):
                    for k in range(KT):
                        mm = pe.matmul(quarter_banks(f"xq{t}", b)[:, g, :], xwq_sb[:, k, g * P:(g + 1) * P],
                                       xnT[:, 1, k, t * P:(t + 1) * P], start=(k == 0), stop=(k == KT - 1))
                mm.then_inc(filled(f"xq{t}", b), 1)

            def cross_out(b, t):
                pe.wait_ge(s_o2T, TT * b + t + 1)
                claim(f"out{t}", b)
                for g in range(HG):
                    mm = pe.matmul(half_banks(f"out{t}", b)[:, 0, :], o2T[:, g, t * P:(t + 1) * P],
                                   xwo_sb[:, g, :], start=(g == 0), stop=(g == HG - 1))
                mm.then_inc(filled(f"out{t}", b), 1)

            def gate_up(b, c, j):
                for w, name in enumerate(("gate", "up")):
                    use = f"{name}{c}{j}"
                    claim(use, b)
                    by_hi = [(wp, x3_hi, k, m) for m in range(2) for k in range(KT) for wp in (wgu_hi, wgu_lo)]
                    by_lo = [(wgu_hi, x3_lo, k, m) for m in range(2) for k in range(KT)]
                    for n, (wp, xp, k, m) in enumerate(by_hi + by_lo):
                        if xp is x3_lo and use == "gate00":
                            wait_drained(pe, "ln3", b)
                        mm = pe.matmul(half_banks(use, b)[:, m, :], wp[:, k, w, c * 4 + 2 * j + m, :],
                                       xp[:, k, :], start=(n == 0), stop=(xp is x3_lo and k == KT - 1),
                                       skip_group_check=True)
                    mm.then_inc(filled(use, b), 1)

            def down(b, c):
                if c == 0:
                    claim("down", b)
                for j in range(4):
                    pe.wait_ge(s_kept, 4 * (FC * b + c) + j + 1)
                    for t in range(TT):
                        mm = pe.matmul(half_banks("down", b)[:, t, :], hidden[:, c, j, t * P:(t + 1) * P],
                                       wd_sb[:, c * 4 + j, :], start=(c == 0 and t == 0 and j == 0),
                                       stop=(c == FC - 1 and j == 3), skip_group_check=True)
                if c == FC - 1:
                    mm.then_inc(filled("down", b), 1)

            def batch(b, more):
                for i in range(HEAD, NQB + LAG_V):
                    if i < NQB:
                        unit_scores(b, i)
                    if LAG_T <= i < NQB + LAG_T:
                        unit_transpose(b, i - LAG_T)
                    if i == NQB + LAG_V - 1 and more:
                        transpose_norm("ln1", b, 3 * b + 2)
                    if i >= NQB:
                        window_out(b, 0, pair=i - NQB)
                    if i >= LAG_V:
                        unit_values(b, i - LAG_V)
                if more:
                    wait_drained(pe, "ln1", b)
                    v_tile("v0", b, 0)
                for p in range(PAIRS):
                    window_out(b, 1, pair=p)
                    if p == 0 and more:
                        v_tile("v1", b, 1)
                if more:
                    rope_group("k0", b, QG)
                n = 3 * b + (3 if more else 2)
                cross_norm(b, 0, n)
                if more:
                    rope_group("k1", b, QG + 1)
                cross_q(b, 0)
                if more:
                    rope_group("q0", b, 0)
                if not more:
                    unit_scores(b, NQB)
                    unit_scores(b, NQB + 1)
                cross_norm(b, 1, n)
                if more:
                    rope_group("q1", b, 1)
                cross_q(b, 1)
                for i in range(XU + LAG_V):
                    if i in X_FILL and more:
                        rope_group(f"q{X_FILL[i]}", b, X_FILL[i])
                    if i < XU and (more or i >= 2):
                        unit_scores(b, NQB + i)
                    if LAG_T <= i < XU + LAG_T:
                        unit_transpose(b, NQB + i - LAG_T)
                    if i == XU + LAG_V - 1 and more:
                        rope_group("q5", b, 5, halves=(0,))
                    if i >= LAG_V:
                        unit_values(b, NQB + i - LAG_V)
                    if i == OUT0_AT:
                        cross_out(b, 0)
                if more:
                    rope_group("q5", b, 5, halves=(1,))
                cross_out(b, 1)
                if more:
                    rope_group("q6", b, 6)
                    rope_group("q7", b, 7)
                transpose_norm("ln3", b, 3 * b + (4 if more else 3))
                if b == 0:
                    pe.wait_ge(s_wlo, WCHUNKS)
                pe.wait_ge(s_x3hi, b + 1)
                for c in range(FC):
                    for j in range(2):
                        gate_up(b, c, j)
                if more:
                    unit_scores(b + 1, 0)
                    latent_kv(b, b + 2)
                down(b, 0)
                if more:
                    unit_scores(b + 1, 1)
                    unit_scores(b + 1, 2)
                down(b, 1)

            pe.wait_ge(s_ident, 16)
            transpose_norm("ln1", None, 1)
            wait_drained(pe, "ln1", None)
            pe.wait_ge(s_wk, 16 * GROUPS)
            rope_group("k0", None, QG)
            rope_group("k1", None, QG + 1)
            pe.wait_ge(s_wv, 16)
            v_tile("v0", None, 0)
            for g in range(QG):
                pe.wait_ge(s_wq[g // 2], 16)
                rope_group(f"q{g}", None, g)
                if g == QG // 2:
                    v_tile("v1", None, 1)
            pe.wait_ge(s_xkv, 16 * 2)
            latent_kv(None, 1)
            pe.wait_ge(s_cbf, 2)
            pe.wait_ge(s_zero, 2)
            for i in range(HEAD):
                unit_scores(0, i)
            pe.wait_ge(s_wo, 16)
            pe.wait_ge(s_xw, 16 * 2)
            pe.wait_ge(s_wd, 16)
            for b in range(B):
                batch(b, b + 1 < B)

        @block.vector
        def _(dve):
            def row_moments(src, which, n, t, addend=None, b=None):
                m = TT * (n - 1) + t + 1
                if addend:
                    use = f"{addend}{t}"
                    wait_filled(dve, use, b)
                    dve.tensor_tensor(src[:, t, :], half_banks(use, b)[:, 0, :], src[:, t, :], ALU.add)\
                       .then_inc(drained(use, b), 1)
                    wait_drained(dve, use, b)
                dve.bn_stats(stats[:, which, t, :], src[:, t, :]).then_inc(s_stats, 1)
                dve.wait_ge(s_stats, m)
                dve.bn_aggr(moments[:, which, t, :], stats[:, which, t, :]).then_inc(s_mom, 1)
                dve.wait_ge(s_mom, m)
                dve.tensor_scalar(vareps[:, which, t:t + 1], moments[:, which, t, 1:2], EPS, None,
                                  ALU.add).then_inc(s_var, 1)

            def normalise(src, which, n, t, prior=None):
                dve.wait_ge(s_rstd, TT * (n - 1) + t + 1)
                if prior:
                    wait_filled(dve, *prior)
                dve.tensor_scalar(xn[:, t, :], src[:, t, :], moments[:, which, t, 0:1],
                                  rstd[:, which, t:t + 1], ALU.subtract, ALU.mult).then_inc(s_xn, 1)

            def rope_group(name, b, g, n):
                wait_filled(dve, name, b)
                if n > 2:
                    dve.wait_ge(s_addP, pool_sums(n - 2))
                src = half_banks(name, b)
                ring = (n - 1) % 2
                cos, sin = rope[:, ring, 0], rope[:, ring, 1]
                for by, to in enumerate((cos, sin)):
                    ins = dve.tensor_tensor(to, src, trig_sb[:, by:by + 1, :].broadcast_to([P, 2, S]), ALU.mult)
                ins.then_inc(drained(name, b), 1)

            def rope_sums(name, b, g, n):
                wait_drained(dve, name, b)
                ring = (n - 1) % 2
                cos, sin = rope[:, ring, 0], rope[:, ring, 1]
                if g < QG:
                    G, r = g // R, g % R
                    for up in range(2):
                        rows = slice(64 * up, 64 * up + 64)
                        ins = dve.tensor_tensor(qs[64:128, 2 * G + up, :, r], cos[rows, 1, :], sin[rows, 0, :],
                                                ALU.add)
                else:
                    G = g - QG
                    for i in range(4):
                        rows = slice(32 * i, 32 * i + 32)
                        to = 64 + 32 * (i % 2)
                        ins = dve.tensor_tensor(kd[to:to + 32, 2 * G + i // 2, i % 2, WIN:], cos[rows, 1, :],
                                                sin[rows, 0, :], ALU.add)
                ins.then_inc(s_addV, 1)

            def unit_shape(i):
                return dict(g=8 if i < NQB else (4 if i - NQB < XU0 else 2))

            def unit_max(b, i):
                u = UNITS * b + i
                g = unit_shape(i)["g"]
                src = ps[:, BANK_S + i % 2, :].rearrange("p (g k) -> p g k", g=g)
                dve.wait_ge(s_score, u + 1)
                if i >= NQB:
                    dve.tensor_reduce(mx[:, i % ND, 0:g], src, AX.X, ALU.max, negate=True).then_inc(s_max, 1)
                    return
                dve.tensor_reduce(mx[:, i % ND, 0:g], src, AX.X, ALU.max).then_inc(s_max, 1)
                dve.wait_ge(s_max, u + 1)
                if u >= ND:
                    dve.wait_ge(s_tr, u - ND + 1)
                dve.tensor_tensor(prob[:, i % ND, :].rearrange("p (g k) -> p g k", g=g), src,
                                  mx[:, i % ND, 0:g].unsqueeze(2).broadcast_to([P, g, 512 // g]),
                                  ALU.subtract).then_inc(s_sub, 1)

            def unit_sum(b, i):
                u = UNITS * b + i
                g = unit_shape(i)["g"]
                dve.wait_ge(s_exp, u + 1)
                if i < NQB:
                    dve.tensor_reduce(total[:, i % ND, 0:g],
                                      prob[:, i % ND, :].rearrange("p (g k) -> p g k", g=g),
                                      AX.X, ALU.add).then_inc(s_sum, 1)
                    dve.wait_ge(s_sum, NQB * b + i + 1)
                if u >= ND:
                    dve.wait_ge(s_norm, u - ND + 1)
                dve.reciprocal(inv[:, i % ND, 0:g], total[:, i % ND, 0:g]).then_inc(s_inv, 1)

            def chunk_values(b, c, j):
                wait_filled(dve, f"up{c}{j}", b)
                wait_drained(dve, f"gate{c}{j}", b)
                h = hidden[:, c, 2 * j:2 * j + 2, :]
                dve.tensor_tensor(h, h, half_banks(f"up{c}{j}", b), ALU.mult)\
                   .then_inc(drained(f"up{c}{j}", b), 1)

            def sparsify(b, c):
                n = FC * b + c + 1
                dve.wait_ge(s_mag, 2 * n)
                dve.tensor_tensor(beats[:, 0:2, :], mag[:, 0::2, :], mag[:, 1::2, :], ALU.is_ge)
                dve.tensor_tensor(beats[:, 2:4, :], mag[:, 0:2, :], mag[:, 2:4, :], ALU.is_ge)
                dve.tensor_tensor(beats[:, 4, :], mag[:, 0, :], mag[:, 3, :], ALU.is_ge)
                dve.tensor_tensor(beats[:, 5, :], mag[:, 1, :], mag[:, 2, :], ALU.is_ge).then_inc(s_beats, 1)
                dve.wait_ge(s_beats, n)
                b01, b23, b02, b13, b03, b12 = (beats[:, k, :] for k in range(6))
                dve.tensor_tensor(part[:, 0:2, :], beats[:, 2:4, :], beats[:, 4:6, :], ALU.add)
                dve.tensor_tensor(part[:, 2, :], b02, b12, ALU.add)
                dve.tensor_tensor(part[:, 3, :], b13, b03, ALU.add).then_inc(s_part, 1)
                dve.wait_ge(s_part, n)
                dve.tensor_tensor(wins[:, 0, :], part[:, 0, :], b01, ALU.add)
                dve.tensor_tensor(wins[:, 1, :], part[:, 1, :], b01, ALU.subtract)
                dve.tensor_tensor(wins[:, 2, :], b23, part[:, 2, :], ALU.subtract)
                dve.tensor_tensor(wins[:, 3, :], part[:, 3, :], b23, ALU.add).then_inc(s_wins, 1)
                dve.wait_ge(s_wins, n)
                for j, (op, least) in enumerate(((ALU.is_ge, 2.0), (ALU.is_ge, 1.0), (ALU.is_ge, 0.0),
                                                 (ALU.is_le, 1.0))):
                    dve.scalar_tensor_tensor(hidden[:, c, j, :], wins[:, j, :], least, hidden[:, c, j, :],
                                             op, ALU.mult).then_inc(s_kept, 1)

            def add_out(b):
                wait_filled(dve, "down", b)
                dve.tensor_tensor(x_res[:], half_banks("down", b), x_res[:], ALU.add)\
                   .then_inc(drained("down", b), 1)

            def next_group(name, b, g, k):
                n = RG * (b + 1) + k
                rope_group(name, b, g, n)
                rope_sums(name, b, g, n)

            def batch(b, more):
                for i in range(HEAD, NQB + LAG_V):
                    if i < NQB:
                        unit_max(b, i)
                    if i <= NQB:
                        unit_sum(b, i - 1)
                if more:
                    dve.wait_ge(s_xln, 16 * (b + 2))
                    for t in range(TT):
                        row_moments(x_ln, 0, 3 * b + 2, t)
                    for t in range(TT):
                        normalise(x_ln, 0, 3 * b + 2, t, ("ln3", b - 1) if b else ("ln1", None))
                dve.wait_ge(s_xres, 16 * (b + 1))
                n = 3 * b + (3 if more else 2)
                for t in range(TT):
                    row_moments(x_res, 1, n, t, "wo", b)
                    normalise(x_res, 1, n, t, ("ln1", b) if more else ("ln3", b - 1))
                    if t == 0 and more:
                        for q in range(NQB):
                            v_blocks(dve, dve.tensor_copy, b, q)
                if more:
                    next_group("k0", b, QG, 1)
                    next_group("k1", b, QG + 1, 2)
                    for g in range(2):
                        next_group(f"q{g}", b, g, 3 + g)
                for i in range(XU + LAG_V):
                    if i < XU:
                        unit_max(b, NQB + i)
                    if 1 <= i <= XU:
                        unit_sum(b, NQB + i - 1)
                    if i in X_FILL and more:
                        next_group(f"q{X_FILL[i]}", b, X_FILL[i], 3 + X_FILL[i])
                    if i == OUT0_AT + 1:
                        row_moments(x_res, 2, n + 1, 0, "out", b)
                    if i == OUT0_AT + 2:
                        normalise(x_res, 2, n + 1, 0, ("ln21", b))
                if more:
                    next_group("q5", b, 5, 8)
                row_moments(x_res, 2, n + 1, 1, "out", b)
                normalise(x_res, 2, n + 1, 1)
                if more:
                    rope_group("q6", b, 6, RG * (b + 1) + 9)
                dve.wait_ge(s_x3hi, b + 1)
                dve.tensor_tensor(x3_lo[:], half_banks("ln3", b), x3_hi[:].bitcast(F32), ALU.subtract)\
                   .then_inc(drained("ln3", b), 1)
                if more:
                    rope_sums("q6", b, 6, RG * (b + 1) + 9)
                    next_group("q7", b, 7, 10)
                for j in range(2):
                    chunk_values(b, 0, j)
                sparsify(b, 0)
                for j in range(2):
                    chunk_values(b, 1, j)
                if more:
                    unit_max(b + 1, 0)
                sparsify(b, 1)
                if more:
                    for i in range(1, HEAD):
                        unit_max(b + 1, i)
                        unit_sum(b + 1, i - 1)
                add_out(b)

            dve.wait_ge(s_xln, 16)
            for t in range(TT):
                row_moments(x_ln, 0, 1, t)
            for t in range(TT):
                normalise(x_ln, 0, 1, t)
            dve.memset(v2z[:], 0.0).then_inc(s_zero, 1)
            dve.wait_ge(s_ident, 16)
            dve.tensor_copy(ident_bf[:], ident_sb[:]).then_inc(s_cbf, 1)
            dve.wait_ge(s_zero, 2)
            dve.wait_ge(s_trig, 16)
            for g in range(GROUPS):
                rope_group(f"k{g}", None, QG + g, g + 1)
                rope_sums(f"k{g}", None, QG + g, g + 1)
            for g in range(QG):
                rope_group(f"q{g}", None, g, GROUPS + g + 1)
                rope_sums(f"q{g}", None, g, GROUPS + g + 1)
                if g == QG // 2:
                    dve.wait_ge(s_masks, 32)
                    dve.tensor_copy(mask_sb[:], mask_f[:]).then_inc(s_cbf, 1)
            unit_max(0, 0)
            for i in range(1, HEAD):
                unit_max(0, i)
                unit_sum(0, i - 1)
            for b in range(B):
                batch(b, b + 1 < B)

        @block.gpsimd
        def _(pool):
            def inverse_root(which, n, tiles=range(TT)):
                for t in tiles:
                    pool.wait_ge(s_var, TT * (n - 1) + t + 1)
                    pool.tensor_tensor(rstd[:, which, t:t + 1], vareps[:, which, t:t + 1], power[:],
                                       ALU.pow).then_inc(s_rstd, 1)

            def rope_sums(name, b, g, n):
                wait_drained(pool, name, b)
                ring = (n - 1) % 2
                cos, sin = rope[:, ring, 0], rope[:, ring, 1]
                done = pool_sums(n - 1)
                if g < QG:
                    G, r = g // R, g % R
                    for up in range(2):
                        if done + up:
                            pool.wait_ge(s_addP, done + up)
                        rows = slice(64 * up, 64 * up + 64)
                        pool.tensor_tensor(qs[0:64, 2 * G + up, :, r], cos[rows, 0, :], sin[rows, 1, :],
                                           ALU.subtract).then_inc(s_addP, 1)
                else:
                    G = g - QG
                    for i in range(4):
                        if done + i:
                            pool.wait_ge(s_addP, done + i)
                        rows = slice(32 * i, 32 * i + 32)
                        to = 32 * (i % 2)
                        pool.tensor_tensor(kd[to:to + 32, 2 * G + i // 2, i % 2, WIN:], cos[rows, 0, :],
                                           sin[rows, 1, :], ALU.subtract).then_inc(s_addP, 1)

            def unit_norm(b, i):
                u = UNITS * b + i
                g = 8 if i < NQB else (4 if i - NQB < XU0 else 2)
                pool.wait_ge(s_inv, u + 1)
                p = prob[:, i % ND, :].rearrange("p (g k) -> p g k", g=g)
                pool.tensor_tensor(p, p, inv[:, i % ND, 0:g].unsqueeze(2).broadcast_to([P, g, 512 // g]),
                                   ALU.mult).then_inc(s_norm, 1)

            def cross_keys(b, h):
                if h == 0:
                    wait_drained(pool, "xk", before(b))
                ins = pool.tensor_tensor(k2d[:, 1, h, :], k2T[:, 1, :],
                                         rowmask_sb[:, h:h + 1].broadcast_to([P, S]), ALU.mult)
                if h == HPT - 1:
                    ins.then_inc(s_k2v, 1)

            def split_weights(c):
                pool.wait_ge(s_whi, c + 1)
                pool.tensor_tensor(lo_c[c], raw[:, c % RAW, :], hi_c[c].bitcast(F32), ALU.subtract)\
                    .then_inc(s_wlo, 1)

            def next_group(name, b, g, k):
                rope_sums(name, b, g, RG * (b + 1) + k)

            def after_sums(b, k):
                pool.wait_ge(s_addP, pool_sums(RG) * (b + 1) + pool_sums(k))

            def batch(b, more):
                after_sums(b, 0)
                for i in range(NQB):
                    unit_norm(b, i)
                    cross_keys(b, i)
                if more:
                    inverse_root(0, 3 * b + 2)
                n = 3 * b + (3 if more else 2)
                inverse_root(1, n, (0,))
                if b == 0:
                    for c in range(SPLITS):
                        split_weights(c)
                inverse_root(1, n, (1,))
                if more:
                    pool.wait_ge(s_rstd, TT * n)
                    next_group("k0", b, QG, 1)
                    next_group("k1", b, QG + 1, 2)
                    for g in range(2):
                        next_group(f"q{g}", b, g, 3 + g)
                    after_sums(b, 4)
                for i in range(XU + LAG_V):
                    if 1 <= i <= XU:
                        unit_norm(b, NQB + i - 1)
                    if i in X_FILL and more:
                        pool.wait_ge(s_norm, UNITS * b + NQB + min(i, XU))
                        g = X_FILL[i]
                        next_group(f"q{g}", b, g, 3 + g)
                        after_sums(b, 3 + g)
                    if i == OUT0_AT + 1:
                        inverse_root(2, n + 1, (0,))
                    if b == 0 and 0 <= i - LAG_V < WCHUNKS - SPLITS:
                        split_weights(SPLITS + i - LAG_V)
                if more:
                    pool.wait_ge(s_norm, UNITS * (b + 1))
                    if b == 0:
                        pool.wait_ge(s_wlo, WCHUNKS)
                    pool.wait_ge(s_rstd, TT * n + 1)
                    next_group("q5", b, 5, 8)
                    after_sums(b, 8)
                inverse_root(2, n + 1, (1,))
                if more:
                    pool.wait_ge(s_rstd, TT * (n + 1))
                    for g in range(6, QG):
                        next_group(f"q{g}", b, g, 3 + g)

            pool.memset(power[:], -0.5).then_inc(s_power, 1)
            pool.wait_ge(s_power, 1)
            inverse_root(0, 1)
            pool.memset(kd[:], 0.0)
            pool.memset(vb[:], 0.0).then_inc(s_zero, 1)
            pool.wait_ge(s_zero, 2)
            for g in range(GROUPS):
                rope_sums(f"k{g}", None, QG + g, g + 1)
            for g in range(QG):
                rope_sums(f"q{g}", None, g, GROUPS + g + 1)
            pool.wait_ge(s_masks, 32)
            for b in range(B):
                batch(b, b + 1 < B)

        @block.scalar
        def _(act):
            def copy_norm(name, b, which):
                wait_filled(act, name, b)
                act.activation(xnT[:, which], half_banks(name, b), ACT.Copy)\
                   .then_inc(drained(name, b), 1)

            def v_copy(name, b, t):
                wait_filled(act, name, b)
                act.activation(v_sb[:, t, :], bank(name, b), ACT.Copy).then_inc(drained(name, b), 1)

            def unit_exp(b, i):
                u = UNITS * b + i
                if i < NQB:
                    act.wait_ge(s_sub, NQB * b + i + 1)
                    act.activation(prob[:, i % ND, :], prob[:, i % ND, :], ACT.Exp, scale=HD ** -0.5)\
                       .then_inc(s_exp, 1)
                    return
                act.wait_ge(s_max, u + 1)
                act.wait_ge(s_tr, u - ND + 1)
                g = 4 if i - NQB < XU0 else 2
                k = 512 // g
                for h in range(g):
                    ins = act.activation(prob[:, i % ND, h * k:(h + 1) * k],
                                         ps[:, BANK_S + i % 2, h * k:(h + 1) * k], ACT.Exp,
                                         bias=mx[:, i % ND, h:h + 1], accum_out=total[:, i % ND, h:h + 1])
                ins.then_inc(s_exp, 1)

            def unit_pT(b, i):
                u = UNITS * b + i
                act.wait_ge(s_tr, u + 1)
                if u >= 2:
                    act.wait_ge(s_av, u - 1)
                act.activation(pT[:, i % 2, :], ps[:, BANK_PT + i % 2, :], ACT.Copy).then_inc(s_pT, 1)

            def unit_out(b, i):
                act.wait_ge(s_av, UNITS * b + i + 1)
                act.activation(qs_rows[:, :, i * P:(i + 1) * P],
                               ps[:, BANK_O, :].rearrange("p (c n) -> p c n", c=PAIRS), ACT.Copy).then_inc(s_oT, 1)

            def cross_outputs(b, t):
                act.wait_ge(s_av, UNITS * b + NQB + (XU0, XU)[t])
                tile = slice(t * P, (t + 1) * P)
                act.activation(o2T[:, :, tile], ps[:, BANK_O, :].rearrange("p (g s) -> p g s", g=HG)[:, :, tile],
                               ACT.Copy).then_inc(s_o2T, 1)

            def latent_kv(b):
                wait_filled(act, "xk", b)
                act.activation(k2T[:], half_banks("xk", b), ACT.Copy).then_inc(drained("xk", b), 1)
                wait_filled(act, "xv", b)
                src = half_banks("xv", b).rearrange("p t (h e d) -> p t h e d", h=XH // 2, e=2)
                for e in range(2):
                    for t in range(TT):
                        ins = act.activation(v2z[:, t, e::2, e * XD:(e + 1) * XD], src[:, t, :, e, :], ACT.Copy)
                ins.then_inc(drained("xv", b), 1)

            def cross_keys(b, h):
                if h == 0:
                    wait_drained(act, "xk", before(b))
                ins = act.activation(k2d[:, 0, h, :], k2T[:, 0, :], ACT.Copy, scale=rowmask_sb[:, h:h + 1])
                if h == HPT - 1:
                    ins.then_inc(s_k2a, 1)

            def round_weights(c):
                act.wait_ge(s_wraw[c % RAW], 16 * (c // RAW + 1))
                act.activation(hi_c[c], raw[:, c % RAW, :], ACT.Copy).then_inc(s_whi, 1)

            def gate(b, c, j):
                use = f"gate{c}{j}"
                wait_filled(act, use, b)
                act.activation(hidden[:, c, 2 * j:2 * j + 2, :], half_banks(use, b), ACT.Silu)\
                   .then_inc(drained(use, b), 1)

            def magnitudes(b, c, j):
                wait_drained(act, f"up{c}{j}", b)
                if c:
                    act.wait_ge(s_beats, FC * b + c)
                act.activation(mag[:, 2 * j:2 * j + 2, :], hidden[:, c, 2 * j:2 * j + 2, :], ACT.Abs)\
                   .then_inc(s_mag, 1)

            def batch(b, more):
                for i in range(HEAD, NQB + LAG_V):
                    if i == NQB + LAG_V - 1 and more:
                        copy_norm("ln1", b, 0)
                    if LAG_T <= i < NQB + LAG_T:
                        unit_pT(b, i - LAG_T)
                    if i >= LAG_V:
                        unit_out(b, i - LAG_V)
                    if i < NQB:
                        unit_exp(b, i)
                    if 3 <= i < 3 + HPT:
                        cross_keys(b, i - 3)
                    if b == 0 and 0 <= i - HEAD < RAW:
                        round_weights(i - HEAD)
                if more:
                    for t in range(TT):
                        v_copy(f"v{t}", b, t)
                if b == 0:
                    for c in range(RAW, WCHUNKS):
                        round_weights(c)
                for t in range(TT):
                    tile = slice(t * P, (t + 1) * P)
                    wait_filled(act, f"ln2{t}", b)
                    act.activation(xnT[:, 1, :, tile], quarter_banks(f"ln2{t}", b)[:, 0:KT, :], ACT.Copy)\
                       .then_inc(drained(f"ln2{t}", b), 1)
                    wait_filled(act, f"xq{t}", b)
                    act.activation(q2T[:, :, tile], quarter_banks(f"xq{t}", b)[:, 0:HG, :], ACT.Copy,
                                   scale=XD ** -0.5).then_inc(drained(f"xq{t}", b), 1)
                for i in range(XU + LAG_T):
                    if i >= LAG_T:
                        unit_pT(b, NQB + i - LAG_T)
                    if i < XU:
                        unit_exp(b, NQB + i)
                    if i == XU0 + LAG_V - 1:
                        cross_outputs(b, 0)
                cross_outputs(b, 1)
                wait_filled(act, "ln3", b)
                act.activation(x3_hi[:], half_banks("ln3", b), ACT.Copy).then_inc(s_x3hi, 1)
                for c in range(FC):
                    for j in range(2):
                        gate(b, c, j)
                    for j in range(2):
                        magnitudes(b, c, j)
                if more:
                    unit_exp(b + 1, 0)
                    latent_kv(b)
                    for i in range(1, HEAD):
                        unit_exp(b + 1, i)
                    wait_filled(act, "down", b)

            copy_norm("ln1", None, 0)
            v_copy("v0", None, 0)
            v_copy("v1", None, 1)
            act.wait_ge(s_zero, 2)
            for q in range(NQB):
                v_blocks(act, act.copy, None, q)
            latent_kv(None)
            act.wait_ge(s_masks, 32)
            for i in range(HEAD):
                unit_exp(0, i)
            for b in range(B):
                batch(b, b + 1 < B)


def constants():
    inv_freq = (1.0 / np.float32(10000.0) ** (np.arange(0, HD, 2, dtype=np.float32) / np.float32(HD)))
    angle = np.arange(S, dtype=np.float32)[:, None] * inv_freq.astype(np.float32)[None, :]
    cos, sin = np.cos(angle).T, np.sin(angle).T
    trig = np.tile(np.stack([cos, sin], axis=1), (4, 1, 1)).astype(np.float32)
    q, k = np.arange(QB)[:, None], np.arange(WK)[None, :]
    hidden = (k > WIN + q) | (k < q)
    first = hidden | (k < WIN)
    later = np.arange(P)[None, :] > np.arange(P)[:, None]
    masks = np.concatenate([np.repeat(first, R, 0), np.repeat(hidden, R, 0), later], axis=1)
    masks = np.where(masks, MASKED, 0.0).astype(np.float32)
    rowmask = (np.arange(P)[:, None] // XD == np.arange(HPT)[None, :]).astype(np.float32)
    return trig, masks, np.eye(P, dtype=np.float32), rowmask


def kernel(x, ctx_512, L0_attn_wq, L0_attn_wk, L0_attn_wv, L0_attn_wo, L0_xattn_Wq, L0_xattn_Wkv_expand,
           L0_xattn_Wout, L0_ffn_w_gate, L0_ffn_w_up, L0_ffn_w_down):
    import concourse.bacc as bacc
    from concourse.bass_utils import run_bass_kernel_spmd

    a = np.asarray
    q = a(L0_attn_wq).reshape(GROUPS, 4, R, 2, HALF, D).transpose(5, 0, 2, 3, 1, 4).reshape(D, QG, 2, P)
    k = a(L0_attn_wk).reshape(GROUPS, 4, 2, HALF, D).transpose(4, 0, 2, 1, 3).reshape(D, GROUPS, 2, P)
    by_k = lambda w: w.reshape(KT, P, *w.shape[1:]).swapaxes(0, 1)
    ffn = lambda w: by_k(a(w).reshape(D, FC, P, 4).transpose(0, 1, 3, 2).reshape(D, FC * 4, P))
    trig, masks, ident, rowmask = constants()
    arrays = {
        "x": a(x),
        "ctxT": a(ctx_512)[:, :S].transpose(0, 2, 1),
        "wqk": by_k(np.concatenate([q, k], axis=1)),
        "wv": by_k(a(L0_attn_wv).T),
        "wo": a(L0_attn_wo).T.reshape(PAIRS, 2, R, HD, D).transpose(1, 3, 0, 2, 4).reshape(P, PAIRS, R, D),
        "xwq": by_k(a(L0_xattn_Wq).T),
        "xwk": a(L0_xattn_Wkv_expand)[:D].T,
        "xwv": a(L0_xattn_Wkv_expand)[D:].T,
        "xwo": by_k(a(L0_xattn_Wout).T),
        "wgu": np.stack([ffn(L0_ffn_w_gate), ffn(L0_ffn_w_up)], axis=2),
        "wd": a(L0_ffn_w_down).reshape(FC, P, 4, D).transpose(1, 0, 2, 3).reshape(P, FC * 4, D),
        "trig": trig, "masks": masks, "ident": ident, "rowmask": rowmask,
    }
    nc = bacc.Bacc("TRN2", target_bir_lowering=False, num_devices=1)
    args, feeds = {}, {}
    for name, v in arrays.items():
        feeds[f"in_{name}"] = np.ascontiguousarray(v)
        args[name] = nc.dram_tensor(f"in_{name}", v.shape, F32, kind="ExternalInput").ap()
    args["out"] = nc.dram_tensor("out_0", (B, S, D), F32, kind="ExternalOutput").ap()
    build(nc, **args)
    r = run_bass_kernel_spmd(nc, [feeds], core_ids=[0])
    return r.results[0]["out_0"]
```
